# Optimizing a Trainium2 kernel written in Bass

```python
import numpy as np
import jax
import jax.numpy as jnp

def _softmax(x, axis=-1):
    return jax.nn.softmax(x, axis=axis)

def _gelu(x):
    return jax.nn.gelu(x, approximate=True)

def _silu(x):
    return jax.nn.silu(x)

def _sigmoid(x):
    return jax.nn.sigmoid(x)

def _layernorm(x, axis=-1, eps=1e-05):
    m = jnp.mean(x, axis=axis, keepdims=True)
    v = jnp.var(x, axis=axis, keepdims=True)
    return (x - m) / jnp.sqrt(v + eps)

def _scatter_add(tgt, idx, src, axis=0):
    return tgt.at[idx].add(src)

def _segment_sum(src, seg, n):
    return jax.ops.segment_sum(src, seg, n)
kernel_name = 'mk_hybrid_d1_jaxref_r8_d49a73'

def setup_inputs(seed: int=0):
    np.random.seed(seed)
    _w = jnp.asarray

    def _L0_attn_a_setup():
        import jax, jax.numpy as jnp
        import numpy as np
        DIM = 256
        HEADS = 16
        HEAD_DIM = DIM // HEADS
        RANK = 16
        ALPHA = 8.0
        SCALING = ALPHA / RANK
        SCALE = HEAD_DIM ** (-0.5)

        def lora_linear(x, W, b, Bm, Am):
            out = jnp.einsum('bld,od->blo', x, W) + b
            upd = jnp.einsum('blr,or->blo', jnp.einsum('bld,rd->blr', x, Bm), Am)
            return out + SCALING * upd

        def _split(t):
            B, L, D = t.shape
            return t.reshape(B, L, HEADS, HEAD_DIM).transpose(0, 2, 1, 3)
        key = jax.random.key(seed)
        ks = jax.random.split(key, 20)
        B, L = (4, 256)
        x = jax.random.normal(ks[0], (B, L, DIM), dtype=jnp.float32)
        s = 0.02
        inp = {'x': x}
        for i, name in enumerate(['q', 'k', 'v', 'o']):
            inp[f'W{name}'] = jax.random.normal(ks[1 + 4 * i], (DIM, DIM), jnp.float32) * s
            inp[f'b{name}'] = jax.random.normal(ks[2 + 4 * i], (DIM,), jnp.float32) * s
            inp[f'B{name}'] = jax.random.normal(ks[3 + 4 * i], (RANK, DIM), jnp.float32) * s
            inp[f'A{name}'] = jax.random.uniform(ks[4 + 4 * i], (DIM, RANK), jnp.float32, -0.1, 0.1)
        return inp
    _L0_attn_a_in = _L0_attn_a_setup()

    def _L0_attn_b_setup():
        import jax, jax.numpy as jnp
        import numpy as np
        import math
        B, S, D = (4, 512, 256)
        H, HEAD_DIM = (16, 48)
        D3 = HEAD_DIM // 3

        def _flash_attention(q, k, v, use_causal_mask=True):
            seq_len = q.shape[-2]
            block_size = min(64, seq_len)
            d = q.shape[-1]
            out = jnp.zeros_like(q)
            for i in range(0, seq_len, block_size):
                qb = q[..., i:i + block_size, :]
                kb = k[..., :i + block_size, :]
                vb = v[..., :i + block_size, :]
                scores = jnp.einsum('...hqd,...hkd->...hqk', qb, kb, precision=jax.lax.Precision.HIGHEST)
                scores = scores / jnp.sqrt(jnp.float32(d))
                if use_causal_mask:
                    mask = jnp.tril(jnp.ones((qb.shape[-2], kb.shape[-2]), dtype=jnp.float32))
                    scores = jnp.where(mask == 0, -1000000000.0, scores)
                w = jax.nn.softmax(scores, axis=-1)
                ob = jnp.einsum('...hqk,...hvd->...hqd', w, vb, precision=jax.lax.Precision.HIGHEST)
                out = out.at[..., i:i + block_size, :].set(ob)
            return out
        key = jax.random.key(seed)
        k0, k1, k2 = jax.random.split(key, 3)
        x = jax.random.normal(k0, (B, S, D), dtype=jnp.float32)
        Wqkv = jax.random.normal(k1, (D, H, HEAD_DIM), dtype=jnp.float32) / math.sqrt(D)
        bqkv = jnp.zeros((H, HEAD_DIM), dtype=jnp.float32)
        Wout = jax.random.normal(k2, (H, D3, D), dtype=jnp.float32) / math.sqrt(H * D3)
        bout = jnp.zeros((D,), dtype=jnp.float32)
        return {'x': x, 'Wqkv': Wqkv, 'bqkv': bqkv, 'Wout': Wout, 'bout': bout}
    _L0_attn_b_in = _L0_attn_b_setup()

    def _L0_ffn_setup():
        import jax, jax.numpy as jnp
        import numpy as np
        EPS = 1e-08

        def _bit_quant(w):
            scale = jnp.maximum(jnp.mean(jnp.abs(w)), EPS)
            w_ternary = jnp.clip(jnp.round(w / scale), -1.0, 1.0)
            return w + jax.lax.stop_gradient(w_ternary - w)
        key = jax.random.key(seed)
        k = jax.random.split(key, 5)
        emb, dff = (256, 1024)
        B, S = (4, 256)
        x = jax.random.normal(k[0], (B, S, emb), dtype=jnp.float32)
        w1 = jax.random.normal(k[1], (dff, emb), dtype=jnp.float32) * 0.02
        b1 = jax.random.normal(k[2], (dff,), dtype=jnp.float32) * 0.02
        w2 = jax.random.normal(k[3], (emb, dff), dtype=jnp.float32) * 0.02
        b2 = jax.random.normal(k[4], (emb,), dtype=jnp.float32) * 0.02
        return {'x': x, 'w1': w1, 'b1': b1, 'w2': w2, 'b2': b2}
    _L0_ffn_in = _L0_ffn_setup()
    _d = {'L0_attn_a_x': _L0_attn_a_in['x'], 'L0_attn_a_Wq': _L0_attn_a_in['Wq'], 'L0_attn_a_bq': _L0_attn_a_in['bq'], 'L0_attn_a_Bq': _L0_attn_a_in['Bq'], 'L0_attn_a_Aq': _L0_attn_a_in['Aq'], 'L0_attn_a_Wk': _L0_attn_a_in['Wk'], 'L0_attn_a_bk': _L0_attn_a_in['bk'], 'L0_attn_a_Bk': _L0_attn_a_in['Bk'], 'L0_attn_a_Ak': _L0_attn_a_in['Ak'], 'L0_attn_a_Wv': _L0_attn_a_in['Wv'], 'L0_attn_a_bv': _L0_attn_a_in['bv'], 'L0_attn_a_Bv': _L0_attn_a_in['Bv'], 'L0_attn_a_Av': _L0_attn_a_in['Av'], 'L0_attn_a_Wo': _L0_attn_a_in['Wo'], 'L0_attn_a_bo': _L0_attn_a_in['bo'], 'L0_attn_a_Bo': _L0_attn_a_in['Bo'], 'L0_attn_a_Ao': _L0_attn_a_in['Ao'], 'L0_attn_b_Wqkv': _L0_attn_b_in['Wqkv'], 'L0_attn_b_bqkv': _L0_attn_b_in['bqkv'], 'L0_attn_b_Wout': _L0_attn_b_in['Wout'], 'L0_attn_b_bout': _L0_attn_b_in['bout'], 'L0_ffn_w1': _L0_ffn_in['w1'], 'L0_ffn_b1': _L0_ffn_in['b1'], 'L0_ffn_w2': _L0_ffn_in['w2'], 'L0_ffn_b2': _L0_ffn_in['b2']}
    _x0 = _d['L0_attn_a_x']
    _d['L0_attn_a_x'] = jax.random.normal(jax.random.fold_in(jax.random.key(seed), 1), (1, 1024, 256), dtype=_x0.dtype)
    del _x0
    return _d

def reference(L0_attn_a_x, L0_attn_a_Wq, L0_attn_a_bq, L0_attn_a_Bq, L0_attn_a_Aq, L0_attn_a_Wk, L0_attn_a_bk, L0_attn_a_Bk, L0_attn_a_Ak, L0_attn_a_Wv, L0_attn_a_bv, L0_attn_a_Bv, L0_attn_a_Av, L0_attn_a_Wo, L0_attn_a_bo, L0_attn_a_Bo, L0_attn_a_Ao, L0_attn_b_Wqkv, L0_attn_b_bqkv, L0_attn_b_Wout, L0_attn_b_bout, L0_ffn_w1, L0_ffn_b1, L0_ffn_w2, L0_ffn_b2):

    def _L0_attn_a_ref(x, Wq, bq, Bq, Aq, Wk, bk, Bk, Ak, Wv, bv, Bv, Av, Wo, bo, Bo, Ao):
        import jax, jax.numpy as jnp
        import numpy as np
        DIM = 256
        HEADS = 16
        HEAD_DIM = DIM // HEADS
        RANK = 16
        ALPHA = 8.0
        SCALING = ALPHA / RANK
        SCALE = HEAD_DIM ** (-0.5)

        def lora_linear(x, W, b, Bm, Am):
            out = jnp.einsum('bld,od->blo', x, W) + b
            upd = jnp.einsum('blr,or->blo', jnp.einsum('bld,rd->blr', x, Bm), Am)
            return out + SCALING * upd

        def _split(t):
            B, L, D = t.shape
            return t.reshape(B, L, HEADS, HEAD_DIM).transpose(0, 2, 1, 3)
        q = _split(lora_linear(x, Wq, bq, Bq, Aq))
        k = _split(lora_linear(x, Wk, bk, Bk, Ak))
        v = _split(lora_linear(x, Wv, bv, Bv, Av))
        scores = jnp.einsum('bhqd,bhkd->bhqk', q, k) * SCALE
        attn = jax.nn.softmax(scores, axis=-1)
        out = jnp.einsum('bhqk,bhkd->bhqd', attn, v)
        B, H, L, hd = out.shape
        out = out.transpose(0, 2, 1, 3).reshape(B, L, H * hd)
        return lora_linear(out, Wo, bo, Bo, Ao)

    def _L0_attn_b_ref(x, Wqkv, bqkv, Wout, bout):
        import jax, jax.numpy as jnp
        import numpy as np
        import math
        B, S, D = (4, 512, 256)
        H, HEAD_DIM = (16, 48)
        D3 = HEAD_DIM // 3

        def _flash_attention(q, k, v, use_causal_mask=True):
            seq_len = q.shape[-2]
            block_size = min(64, seq_len)
            d = q.shape[-1]
            out = jnp.zeros_like(q)
            for i in range(0, seq_len, block_size):
                qb = q[..., i:i + block_size, :]
                kb = k[..., :i + block_size, :]
                vb = v[..., :i + block_size, :]
                scores = jnp.einsum('...hqd,...hkd->...hqk', qb, kb, precision=jax.lax.Precision.HIGHEST)
                scores = scores / jnp.sqrt(jnp.float32(d))
                if use_causal_mask:
                    mask = jnp.tril(jnp.ones((qb.shape[-2], kb.shape[-2]), dtype=jnp.float32))
                    scores = jnp.where(mask == 0, -1000000000.0, scores)
                w = jax.nn.softmax(scores, axis=-1)
                ob = jnp.einsum('...hqk,...hvd->...hqd', w, vb, precision=jax.lax.Precision.HIGHEST)
                out = out.at[..., i:i + block_size, :].set(ob)
            return out
        qkv = jnp.einsum('bsm,mhd->bshd', x, Wqkv, precision=jax.lax.Precision.HIGHEST) + bqkv
        q, k, v = jnp.split(qkv, 3, axis=-1)
        attn = _flash_attention(q, k, v, use_causal_mask=True)
        y = jnp.einsum('bshd,hdm->bsm', attn, Wout, precision=jax.lax.Precision.HIGHEST) + bout
        return y

    def _L0_ffn_ref(x, w1, b1, w2, b2):
        import jax, jax.numpy as jnp
        import numpy as np
        EPS = 1e-08

        def _bit_quant(w):
            scale = jnp.maximum(jnp.mean(jnp.abs(w)), EPS)
            w_ternary = jnp.clip(jnp.round(w / scale), -1.0, 1.0)
            return w + jax.lax.stop_gradient(w_ternary - w)
        w1q = _bit_quant(w1)
        w2q = _bit_quant(w2)
        h = jnp.einsum('bsd,fd->bsf', x, w1q) + b1
        h = jax.nn.gelu(h, approximate=False)
        return jnp.einsum('bsf,df->bsd', h, w2q) + b2
    x = L0_attn_a_x
    x = x + _L0_attn_a_ref(_layernorm(x, axis=-1), L0_attn_a_Wq, L0_attn_a_bq, L0_attn_a_Bq, L0_attn_a_Aq, L0_attn_a_Wk, L0_attn_a_bk, L0_attn_a_Bk, L0_attn_a_Ak, L0_attn_a_Wv, L0_attn_a_bv, L0_attn_a_Bv, L0_attn_a_Av, L0_attn_a_Wo, L0_attn_a_bo, L0_attn_a_Bo, L0_attn_a_Ao)
    x = x + _L0_ffn_ref(_layernorm(x, axis=-1), L0_ffn_w1, L0_ffn_b1, L0_ffn_w2, L0_ffn_b2)
    x = x + _L0_attn_b_ref(_layernorm(x, axis=-1), L0_attn_b_Wqkv, L0_attn_b_bqkv, L0_attn_b_Wout, L0_attn_b_bout)
    x = x + _L0_ffn_ref(_layernorm(x, axis=-1), L0_ffn_w1, L0_ffn_b1, L0_ffn_w2, L0_ffn_b2)
    return x

_drawn_inputs = setup_inputs


def setup_inputs(seed=0):
    import zlib

    import numpy as np

    out = dict(_drawn_inputs(seed))
    spreads = {'L0_attn_b_bqkv': (0.0, 0.8), 'L0_attn_b_bout': (0.0, 2.0)}
    factors = {'L0_attn_a_Wq': 8.0,
     'L0_attn_a_bq': 8.0,
     'L0_attn_a_Bq': 8.0,
     'L0_attn_a_Aq': 8.0,
     'L0_attn_a_Wk': 8.0,
     'L0_attn_a_bk': 64.0,
     'L0_attn_a_Bk': 8.0,
     'L0_attn_a_Ak': 8.0,
     'L0_attn_a_Wv': 8.0,
     'L0_attn_a_bv': 8.0,
     'L0_attn_a_Bv': 8.0,
     'L0_attn_a_Av': 8.0,
     'L0_attn_a_Wo': 8.0,
     'L0_attn_a_bo': 31.456,
     'L0_attn_a_Bo': 8.0,
     'L0_attn_a_Ao': 8.0,
     'L0_attn_b_Wqkv': 4.594,
     'L0_attn_b_Wout': 4.584,
     'L0_ffn_b1': 30.608,
     'L0_ffn_b2': 64.0}
    for name, (base, spread) in spreads.items():
        noise = np.random.default_rng([zlib.crc32(name.encode()), seed]).standard_normal(out[name].shape)
        drawn = base * np.exp(spread * noise) if base else spread * noise
        out[name] = jnp.asarray(drawn.astype(out[name].dtype))
    for name, factor in factors.items():
        out[name] = (out[name] * factor).astype(out[name].dtype)
    return out
```

```python
from contextlib import ExitStack

import concourse.bass as bass
from concourse import mybir

F32 = mybir.dt.float32
BF16 = mybir.dt.bfloat16
F16 = mybir.dt.float16
U32 = mybir.dt.uint32
ALU = mybir.AluOpType
ACT = mybir.ActivationFunctionType
AX_X = mybir.AxisListType.X

P = 128
T, D, H, HD, RANK, FF = 1024, 256, 16, 16, 16, 1024
TT = T // P
PAIRS = TT // 2
DC = D // P
FC = FF // P
HC = P // HD
G = 4
NG = H // G
HALF = T // 2
NU = NG * 2
NPART = 3
NTERM = 7
ROWS = NTERM * HD
SROWS = ROWS + NPART
STEPS = TT * G
FILLS = G * TT // 2
LEAD = 5
LORA_SCALE = 8.0 / RANK
SCALE = HD ** -0.5
EPS = 1e-5
NEG = -1e9
WQ_EPS = 1e-8
X_SCALE = 2048.0
K_, Q_, V_, O_ = range(4)

PAIR_BANKS = (0, 2)
SCORE_BANKS = (4, 5)
PV_BANK = 6
SHIFT_BANK = 7
SETUP_BANKS = (4, 5, 6, 7)
TAIL_BANKS = (0, 2, 4, 5, 6, 7)

ITEMS = [(K_, 0, 0), (K_, 0, 1), (Q_, 0, 0), (Q_, 0, 1), (K_, 1, 0), (K_, 1, 1), (Q_, 1, 0), (Q_, 1, 1)]
EARLY_ITEMS = 6


def setup_order():
    yield ("at",)
    for m in range(4):
        yield ("wt", m)
        yield ("lnt", 0, m)
    for i in range(EARLY_ITEMS):
        yield ("proj", i)


def beside_max_pass():
    return [("proj", i) for i in range(EARLY_ITEMS, len(ITEMS))] + [("v", t) for t in range(TT)] + [("wsum",)]


QUADS = H // 4
POOL_QUADS = (3, 2)


def finish_tile(r, t):
    k = r + 1
    if k < 4:
        if t % 2 == 1:
            yield ("var", k, t // 2)


def last_norm(k, s):
    yield ("norm", k, 2 * s + 1)
    yield ("lnt", k, 2 * s)
    yield ("lnt", k, 2 * s + 1)


def attention_out(s):
    t0 = 4 * s
    for i in range(t0, t0 + 6):
        if i < t0 + 4:
            yield ("ao_t", i)
        if t0 <= i - 1 < t0 + 4:
            yield ("o", "a", i - 1)
        if t0 <= i - 2:
            yield ("ao_y", i - 2)
            yield from finish_tile(0, i - 2)
        if i == t0 + 4:
            yield ("norm", 1, 2 * s)
    yield from last_norm(1, s)


def ffn(r, s):
    k = 2 * r + 1
    for f in range(FC + 2):
        if f < FC:
            yield ("h", r, s, f)
        if 0 <= f - 1 < FC:
            yield ("g", r, s, f - 1)
        if 0 <= f - 2:
            yield ("g2", r, s, f - 2)
    for t in range(4 * s, 4 * s + 4):
        yield ("y", r, t)
        yield from finish_tile(k, t)
        if k < 3 and t % 4 == 3:
            yield ("norm", k + 1, 2 * s)
    if k < 3:
        yield from last_norm(k + 1, s)


def head_attention(s):
    t0 = 4 * s
    yield ("qkv", t0)
    for i in range(t0, t0 + 6):
        if i < t0 + 3:
            yield ("qkv", i + 1)
        for n in range(QUADS):
            if i < t0 + 4:
                yield ("s", i, QUADS - 1 - n)
        if i < t0 + 4:
            yield ("soft", i)
        if t0 <= i - 1 < t0 + 4:
            yield ("div", i - 1)
            yield ("o", "b", i - 1)
        if t0 <= i - 2:
            yield ("bo_y", i - 2)
            yield from finish_tile(2, i - 2)
        if i == t0 + 4:
            yield ("norm", 3, 2 * s)
    yield from last_norm(3, s)


def merged(a, b):
    a, b = list(a), list(b)
    out, i, j = [], 0, 0
    while i < len(a) or j < len(b):
        if j >= len(b) or (i < len(a) and i * len(b) <= j * len(a)):
            out.append(a[i])
            i += 1
        else:
            out.append(b[j])
            j += 1
    return out


def tail_events():
    yield from (("w", n) for n in range(4))
    yield from attention_out(0)
    yield from merged(attention_out(1), ffn(0, 0))
    yield from merged(ffn(0, 1), head_attention(0))
    yield from merged(head_attention(1), ffn(1, 0))
    yield from ffn(1, 1)


def tail_order():
    for e in tail_events():
        if e[0] == "w":
            yield ("w1t" if e[1] % 2 == 0 else "w2t", e[1] // 2)
        elif e[0] == "qkv":
            yield ("qk", e[1])
            yield ("kv", e[1])
        elif e[0] in ("ao_t", "o", "ao_y", "lnt", "h", "y", "bo_y"):
            yield e


def numbered():
    of, count = {}, {}
    events = [(kind, 0, p) for kind in ("var", "norm", "lnt") for p in range(PAIRS)]
    for e in [*events, *tail_events()]:
        of[e] = count.get(e[0], 0)
        count[e[0]] = of[e] + 1
    return of


class Banks:

    def __init__(self):
        self.count = [0] * 8
        self.of = {}

    def claim(self, key, bank):
        self.of[key] = (bank, self.count[bank])
        self.count[bank] += 1


def plan_banks():
    banks = Banks()
    for n, key in enumerate([*setup_order(), *beside_max_pass()]):
        banks.claim(key, SETUP_BANKS[n % len(SETUP_BANKS)])
    base = list(banks.count)
    for b in PAIR_BANKS:
        banks.count[b] += NU * FILLS // 2
    for b in SCORE_BANKS:
        banks.count[b] += NU * STEPS // 2
    for b in (PV_BANK, SHIFT_BANK):
        banks.count[b] += NU
    for n, key in enumerate(tail_order()):
        banks.claim(key, TAIL_BANKS[n % len(TAIL_BANKS)])
    return banks.of, base


def build(nc, a):
    uses, base = plan_banks()
    number = numbered()
    events = list(tail_events())
    norms = [e for e in number if e[0] == "norm"]
    kparts_dram = nc.dram_tensor("k_parts", [NPART, DC, P, T], BF16, kind="Internal").ap()
    qparts_dram = nc.dram_tensor("q_parts", [NPART, 2, DC, P, HALF], BF16, kind="Internal").ap()

    with ExitStack() as ctx:
        def sb(name, shape, dt=F32):
            return ctx.enter_context(nc.sbuf_tensor(name, shape, dt))

        def sem(name):
            return ctx.enter_context(nc.semaphore(name))

        x_res = sb("x_res", [P, TT, D])
        xn = sb("xn", [P, 2, 2, D])
        xT = sb("xT", [P, DC, T])
        w_nat = sb("w_nat", [P, 4, DC, D])
        wT = sb("wT", [P, 4, DC, D])
        a_all = sb("a_all", [P, DC, 4, 32])
        b_all = sb("b_all", [P, D])
        aT = sb("aT", [P, D])
        cut = sb("cut", [P, 2, HALF])
        parts = sb("parts", [P, 12 * 1024], BF16)
        k_parts = parts[:, 0:6144].rearrange("p (c a t) -> p c a t", c=DC, a=NPART)
        q_parts = parts[:, 6144:12288].rearrange("p (c h a t) -> p c h a t", c=DC, h=2, a=NPART)
        o_un = parts[:, 0:8192].bitcast(F32).rearrange("p (g t) -> p g t", g=NG)
        pack = sb("pack", [P, 32 * 1024], BF16)
        k_rows = pack[:, 0:16384].rearrange("p (h t) -> p h t", h=H)
        q_rows = pack[:, 16384:32768].rearrange("p (s h t) -> p s h t", s=2, h=H)
        g_parts = pack[:, 0:24576].rearrange("p (a f t) -> p a f t", a=NPART, f=FC)
        g_full = pack[:, 24576:28672].bitcast(F32).rearrange("p (r t) -> p r t", r=4)
        qkv_rooms = wT[:, 0:3, :, :].rearrange("p m c d -> p (m c d)")
        qkv = [room.rearrange("p (h n) -> p h n", h=H)
               for room in (qkv_rooms[:, 0:768], qkv_rooms[:, 768:1536],
                            cut[:, :, :].rearrange("p a t -> p (a t)")[:, 0:768])]
        v_sb = sb("v_sb", [P, TT, H, HD])
        x12 = v_sb[:, :, :, :].rearrange("p t h d -> p (t h d)").bitcast(F16).rearrange("p (n c t) -> p n c t", n=2, c=DC)
        v_slot = sb("v_slot", [P, 2, TT, G, 32])
        pbuf = sb("pbuf", [P, 2, G, HALF])
        pflat = pbuf[:, :, :, :].rearrange("p a g t -> p (a g t)")
        prod = pflat[:, 0:3072].rearrange("p (r n) -> p r n", r=3)
        prod_own = {1: pflat[:, 3072:3584], 0: pflat[:, 3584:3840]}
        late = parts[:, 8192:12288].bitcast(F32)
        o_norm = late[:, 0:512].rearrange("p (r n) -> p r n", r=2)
        oT = late[:, 512:1024].rearrange("p (r c t) -> p r c t", r=2, c=DC)
        probs = late[:, 1024:1536].rearrange("p (r i j) -> p r i j", r=2, i=H)
        s_raw = sb("s_raw", [P, 2, H, H])
        w_out = sb("w_out", [P, DC, D])
        wqkv = w_nat[:, 0:3, :, :].rearrange("p m c d -> p (m c d)").rearrange("p (c n) -> p c n", c=DC)
        bqkv = sb("bqkv", [1, H * 3 * HD])
        w1_nat = sb("w1_nat", [P, FC, D])
        w2_nat = sb("w2_nat", [P, DC, FF])
        w1T = w1_nat[:, 0:4, :].rearrange("p f d -> p (f d)").bitcast(F16).rearrange("p (c f) -> p c f", c=DC)
        w2T = w2_nat[:, 0:1, :].rearrange("p c f -> p (c f)").bitcast(BF16).rearrange("p (f d) -> p f d", f=FC)
        tern1 = sb("tern1", [P, FC, D], BF16)
        tern2 = sb("tern2", [P, DC, FF], BF16)
        below = sb("below", [P, 512], BF16)
        above = sb("above", [P, 512], BF16)
        ident = sb("ident", [P, P])
        identb = sb("identb", [P, P], BF16)
        ones = sb("ones", [P, P])
        onesb = sb("onesb", [P, HALF], BF16)
        causal = sb("causal", [P, H, H])
        kq_bias = sb("kq_bias", [P, 2, DC])
        b1_col = sb("b1_col", [P, FC])
        rows = sb("rows", [P, 3, D])
        bv_row = sb("bv_row", [1, D])
        stats = sb("stats", [P, TT, 6])
        mv = sb("mv", [P, TT, 2])
        rstd = sb("rstd", [P, TT])
        minus_half = sb("minus_half", [P, 2])
        abs_sum = sb("abs_sum", [P, 2])
        thr = sb("thr", [P, 2, 2])
        mx = sb("mx", [P, 2, G * TT // 2])
        mrest = sb("mrest", [P, G * TT // 2])
        m_parts = sb("m_parts", [P, P], BF16)
        m_rows = sb("m_rows", [P, P], BF16)
        rsum = sb("rsum", [P, 2, H])
        hmax = sb("hmax", [P, H])
        hsum = sb("hsum", [P, H])
        w_sum = sb("w_sum", [P, H])
        v_sum = sb("v_sum", [P, HD])

        ps = ctx.enter_context(nc.psum_tensor("ps", [P, 8, 512], F32))

        filled = [sem(f"filled{b}") for b in range(8)]
        drained = [sem(f"drained{b}") for b in range(8)]
        x_in = [sem(f"x_in{p}") for p in range(PAIRS)]
        w_in = [sem(f"w_in{m}") for m in range(4)]
        ab_padded = sem("ab_padded")
        ab_in = sem("ab_in")
        bias_scaled = sem("bias_scaled")
        wout_in = sem("wout_in")
        pv_chunk = sem("pv_chunk")
        kq_bias_in = sem("kq_bias_in")
        bv_in = sem("bv_in")
        rows_in = sem("rows_in")
        cols_in = sem("cols_in")
        w1_in = sem("w1_in")
        w2_in = sem("w2_in")
        wqkv_in = sem("wqkv_in")
        ones_rows_in = sem("ones_rows_in")
        consts = sem("consts")
        pads = sem("pads")
        stats_ready = sem("stats_ready")
        rstd_ready = sem("rstd_ready")
        xn_ready = sem("xn_ready")
        bias_added = sem("bias_added")
        rest_ready = sem("rest_ready")
        part_ready = sem("part_ready")
        parts_out = [sem(f"parts_out{i}") for i in range(6)]
        k_packed = [sem(f"k_packed{i}") for i in range(3)]
        q_packed = [sem(f"q_packed{i}") for i in range(5)]
        dve_step = sem("dve_step")
        pool_step = sem("pool_step")
        max_step = sem("max_step")
        shift_split = sem("shift_split")
        shift_landed = sem("shift_landed")
        v_slot_ready = sem("v_slot_ready")
        abs_ready = sem("abs_ready")
        tern_ready = sem("tern_ready")
        x1_ready = sem("x1_ready")
        g_rest = sem("g_rest")
        g2_ready = sem("g2_ready")
        g3_ready = sem("g3_ready")
        products = sem("products")
        reduced = sem("reduced")
        shifted = sem("shifted")
        exped = sem("exped")
        divided = sem("divided")
        stored = sem("stored")

        def bank(key):
            return ps[:, uses[key][0], :]

        def to_fill(pe, key):
            b, n = uses[key]
            if n:
                pe.wait_ge(drained[b], n)
            return ps[:, b, :]

        def is_filled(eng, key):
            b, n = uses[key]
            eng.wait_ge(filled[b], n + 1)
            return ps[:, b, :]

        def is_drained(eng, key):
            b, n = uses[key]
            eng.wait_ge(drained[b], n + 1)

        def fill_sem(key):
            return filled[uses[key][0]]

        def drain_sem(key):
            return drained[uses[key][0]]

        def factors(t, quad, out):
            nj, i = 4 * quad + 4, slice(4 * quad, 4 * quad + 4)
            shape = [P, 4, nj, HD]
            in0 = qkv[t % 3][:, i, 0:HD].unsqueeze(2).broadcast_to(shape)
            in1 = qkv[t % 3][:, 0:nj, HD:2 * HD].unsqueeze(1).broadcast_to(shape)
            return in0, in1, out[:, 0:4 * nj * HD].rearrange("p (i j n) -> p i j n", i=4, j=nj)

        block = ctx.enter_context(nc.Block())

        @block.sync
        def _(sp):
            xv = a["L0_attn_a_x"].rearrange("o (t p) d -> (o p) t d", p=P)
            for p in range(PAIRS):
                sp.dma_start(x_res[:, 2 * p:2 * p + 2, :], xv[:, 2 * p:2 * p + 2, :]).then_inc(x_in[p], 16)
            for m, name in ((V_, "Wv"), (O_, "Wo")):
                sp.dma_start(w_nat[:, m, :, :],
                             a[f"L0_attn_a_{name}"].rearrange("(c p) d -> p c d", p=P)).then_inc(w_in[m], 16)
            sp.dma_start(bv_row[:, :], a["L0_attn_a_bv"].rearrange("(a n) -> a n", a=1)).then_inc(bv_in, 16)
            for n, name in enumerate(("L0_attn_a_bo", "L0_ffn_b2", "L0_attn_b_bout")):
                sp.dma_start(rows[:, n, :], bass.AP(a[name].tensor, 0, [[0, P], [1, D]])).then_inc(rows_in, 16)
            sp.dma_start(bqkv[:, :], a["L0_attn_b_bqkv"].rearrange("(a h) n -> a (h n)", a=1)).then_inc(wqkv_in, 16)
            sp.dma_start(w_out[:, :, :], a["L0_attn_b_Wout"].rearrange("h d m -> (h d) m")
                         .rearrange("(c p) m -> p c m", p=P)).then_inc(wout_in, 16)
            sp.wait_ge(consts, 4)
            for j in range(NPART):
                sp.dma_start(k_rows[ROWS + j:ROWS + j + 1, :, :].rearrange("o h t -> o (h t)"),
                             onesb[0:H * T // HALF, :]).then_inc(ones_rows_in, 16)

            def store_k(n, c):
                sp.wait_ge(part_ready, 2 if c == 0 else 6)
                sp.dma_start(kparts_dram[:, c, :, :].rearrange("a f t -> f a t"), k_parts[:, c, :, :]) \
                    .then_inc(parts_out[n], 16)

            def store_q(n, c, s):
                sp.wait_ge(part_ready, ITEMS.index((Q_, c, s)) + 1)
                sp.dma_start(qparts_dram[:, s, c, :, :].rearrange("a f t -> f a t"), q_parts[:, c, s, :, :]) \
                    .then_inc(parts_out[n], 16)

            def pack_k(n, c, h0, nh, done):
                sp.wait_ge(parts_out[n], 16)
                at = kparts_dram[0:1, c:c + 1, :, :].offset + h0 * T
                for row, first, count in ((0, 0, 3), (3, 0, 3), (6, 0, 1)):
                    src = bass.AP(kparts_dram.tensor, at + first * DC * P * T,
                                  [[DC * P * T, count], [HC * T, HD], [1, nh * T]])
                    sp.dma_start(k_rows[row * HD:(row + count) * HD, HC * c + h0:HC * c + h0 + nh, :]
                                 .rearrange("p h t -> p (h t)"), src).then_inc(done, 16)

            def pack_q(n, c, s, h0, nh, done):
                sp.wait_ge(parts_out[n], 16)
                at = qparts_dram[0:1, s:s + 1, c:c + 1, :, :].offset + h0 * HALF
                for row, part, count in ((0, 0, 3), (3, 1, 3), (6, 2, 1)):
                    src = bass.AP(qparts_dram.tensor, at + part * 2 * DC * P * HALF,
                                  [[0, count], [HC * HALF, HD], [1, nh * HALF]])
                    sp.dma_start(q_rows[row * HD:(row + count) * HD, s, HC * c + h0:HC * c + h0 + nh, :]
                                 .rearrange("p h t -> p (h t)"), src).then_inc(done, 16)

            store_k(0, 0)
            pack_k(0, 0, 0, G, k_packed[0])
            store_q(1, 0, 0)
            pack_q(1, 0, 0, 0, G, q_packed[0])
            store_q(2, 0, 1)
            pack_q(2, 0, 1, 0, HC, q_packed[1])
            pack_k(0, 0, G, G, k_packed[1])
            pack_q(1, 0, 0, G, G, q_packed[2])
            store_k(3, 1)
            pack_k(3, 1, 0, HC, k_packed[2])
            store_q(4, 1, 0)
            pack_q(4, 1, 0, 0, HC, q_packed[3])
            store_q(5, 1, 1)
            pack_q(5, 1, 1, 0, HC, q_packed[4])

            def land_shift(g, qh, u):
                sp.wait_ge(drained[SHIFT_BANK], base[SHIFT_BANK] + u + 1)
                n = G * TT // 2
                for j in range(NPART):
                    sp.dma_start(q_rows[ROWS + j:ROWS + j + 1, qh, bass.ds(g * G, G), :]
                                 .rearrange("o h t -> o (h t)"), m_rows[n * j:n * j + n, :]) \
                        .then_inc(shift_landed, 16)

            land_shift(0, 0, 0)
            with sp.Fori(0, NG - 1) as g:
                land_shift(g, 1, g * 2 + 1)
                land_shift(g + 1, 0, g * 2 + 2)
            land_shift(NG - 1, 1, NU - 1)

            ov = a["out"].rearrange("o (t p) d -> (o p) t d", p=P)
            for p in range(PAIRS):
                for t in (2 * p, 2 * p + 1):
                    is_drained(sp, ("y", 1, t))
                sp.dma_start(ov[:, 2 * p:2 * p + 2, :], x_res[:, 2 * p:2 * p + 2, :]).then_inc(stored, 16)
            sp.wait_ge(stored, 16 * PAIRS)

        @block.gpsimd
        def _(pool):
            steps = [0]

            def link(ins):
                steps[0] += 1
                ins.then_inc(pool_step, 1)
                pool.wait_ge(pool_step, steps[0])

            def eye(t):
                link(pool.memset(t[:, :], 0.0))
                pool.affine_select(out=t[:, :], in_=t[:, :], compare_op=ALU.not_equal, fill=1.0, base=0,
                                   pattern=[[-1, P]], channel_multiplier=1).then_inc(consts, 1)

            pool.memset(minus_half[:, :], -0.5).then_inc(consts, 1)
            eye(ident)
            pool.memset(ones[:, :], 1.0).then_inc(consts, 1)
            pool.memset(onesb[:, :], 1.0).then_inc(consts, 1)
            eye(identb)

            pool.wait_ge(consts, 5)

            def inverse_deviations(k, p):
                pool.wait_ge(stats_ready, number["var", k, p] + 1)
                pool.tensor_tensor(rstd[:, 2 * p:2 * p + 2], rstd[:, 2 * p:2 * p + 2], minus_half[:, :], ALU.pow) \
                    .then_inc(rstd_ready, 1)

            def add_bias(r, p):
                pool.wait_ge(xn_ready, number["norm", r, p] + 1)
                if r == 0 and p == 0:
                    pool.wait_ge(rows_in, 48)
                row = (0, 1, 2, 1)[r]
                for t in (2 * p, 2 * p + 1):
                    pool.tensor_tensor(x_res[:, t, :], x_res[:, t, :], rows[:, row, :], ALU.add).then_inc(bias_added, 1)

            for p in range(PAIRS):
                inverse_deviations(0, p)

            def third_part(i):
                m, c, s = ITEMS[i]
                dst = k_parts[:, c, 2, HALF * s:HALF * s + HALF] if m == K_ else q_parts[:, c, s, 2, :]
                mid = k_parts[:, c, 1, HALF * s:HALF * s + HALF] if m == K_ else q_parts[:, c, s, 1, :]
                pool.wait_ge(rest_ready, i + 1)
                pool.tensor_tensor(dst, cut[:, i % 2, :], mid, ALU.subtract).then_inc(part_ready, 1)

            for i in range(EARLY_ITEMS):
                third_part(i)
            pool.memset(v_slot[:, :, :, :, HD:32], 1.0).then_inc(pads, 1)
            for i in range(EARLY_ITEMS, len(ITEMS)):
                third_part(i)
            pool.memset(s_raw[:, :, :, :], 0.0).then_inc(pads, 1)
            link(pool.memset(causal[:, :, :], 0.0))
            pool.affine_select(out=causal[:, :, :], in_=causal[:, :, :], compare_op=ALU.is_ge, fill=NEG, base=0,
                               pattern=[[1, H], [-1, H]], channel_multiplier=0).then_inc(consts, 1)
            for p in range(PAIRS):
                add_bias(0, p)


            is_drained(pool, ("wsum",))
            for n, (w, tern) in enumerate(((w1_nat, tern1), (w2_nat, tern2))):
                wf = w[:, :, :].rearrange("p c d -> p (c d)")
                tf = tern[:, :, :].rearrange("p c d -> p (c d)")
                for c in range(4):
                    v = slice(512 * c, 512 * c + 512)
                    link(pool.tensor_scalar(below[:, :], wf[:, v], thr[:, n, 1:2], None, ALU.is_lt))
                    link(pool.tensor_scalar(above[:, :], wf[:, v], thr[:, n, 0:1], None, ALU.is_gt))
                    pool.tensor_tensor(tf[:, v], above[:, :], below[:, :], ALU.subtract).then_inc(tern_ready, 1)
                    pool.wait_ge(tern_ready, 4 * n + c + 1)

            def third_gelu_part(r, s, f):
                n = number["g2", r, s, f]
                pool.wait_ge(g2_ready, n + 1)
                v = slice(HALF * s, HALF * s + HALF)
                pool.tensor_tensor(g_parts[:, 2, f, v], g_full[:, n % 4, :], g_parts[:, 1, f, v], ALU.subtract) \
                    .then_inc(g3_ready, 1)

            made = [0]

            def product(t, quad):
                if made[0] >= 3:
                    pool.wait_ge(reduced, made[0] - 2)
                in0, in1, out = factors(t, quad, prod[:, made[0] % 3, :])
                pool.tensor_tensor(out, in0, in1, ALU.mult).then_inc(products, 1)
                made[0] += 1

            for e in events:
                if e[0] == "var":
                    inverse_deviations(*e[1:])
                if e[0] == "norm":
                    add_bias(*e[1:])
                if e[0] == "g2":
                    third_gelu_part(*e[1:])
                if e[0] == "s" and e[2] in POOL_QUADS:
                    if e[2] == QUADS - 1:
                        is_drained(pool, ("kv", e[1]))
                    product(e[1], e[2])

        @block.scalar
        def _(act):
            for m, name in ((K_, "Wk"), (Q_, "Wq")):
                act.dma_start(w_nat[:, m, :, :],
                              a[f"L0_attn_a_{name}"].rearrange("(c p) d -> p c d", p=P)).then_inc(w_in[m], 16)
            act.wait_ge(ab_padded, 1)
            for m, n in ((K_, "k"), (Q_, "q"), (V_, "v"), (O_, "o")):
                act.dma_start(a_all[:, :, m, 0:RANK], a[f"L0_attn_a_A{n}"].rearrange("(c p) r -> p c r", p=P)) \
                    .then_inc(ab_in, 16)
                act.dma_start(b_all[32 * m:32 * m + RANK, :], a[f"L0_attn_a_B{n}"]).then_inc(ab_in, 16)
            for n, name in enumerate(("bk", "bq")):
                t = a[f"L0_attn_a_{name}"].tensor
                for c in range(DC):
                    act.dma_start(kq_bias[:, n, c:c + 1], bass.AP(t, P * c, [[1, HD], [HD, HC], [1, 1]]),
                                  allow_slow_non_contiguous=True) \
                        .then_inc(kq_bias_in, 16)
            act.dma_start(w1_nat[:, :, :], a["L0_ffn_w1"].rearrange("(f p) d -> p f d", p=P)).then_inc(w1_in, 16)
            act.dma_start(w2_nat[:, :, :], a["L0_ffn_w2"].rearrange("(c p) f -> p c f", p=P)).then_inc(w2_in, 16)

            is_filled(act, ("at",))
            act.mul(aT[:, :], bank(("at",))[:, 0:D], LORA_SCALE).then_inc(drain_sem(("at",)), 1)

            def evacuate_lnt(k, p):
                src = is_filled(act, ("lnt", k, p)).rearrange("p (c t) -> p c t", c=DC)
                act.copy(xT[:, :, 256 * p:256 * p + 256], src).then_inc(drain_sem(("lnt", k, p)), 1)

            for m in range(4):
                key = ("wt", m)
                src = is_filled(act, key)
                if m in (K_, Q_):
                    for c in range(DC):
                        ins = act.copy(wT[:, m, c, :].rearrange("p (f d h) -> p f d h", f=DC, d=HD),
                                       src[:, D * c:D * c + D].rearrange("p (f h d) -> p f d h", f=DC, h=HC))
                else:
                    ins = act.copy(wT[:, m, :, :], src.rearrange("p (c n) -> p c n", c=DC))
                ins.then_inc(drain_sem(key), 1)
                evacuate_lnt(0, m)
            act.dma_start(wqkv[:, :, :], a["L0_attn_b_Wqkv"].rearrange("(c p) h n -> p c (h n)", p=P)).then_inc(wqkv_in, 16)
            act.dma_start(b1_col[:, :], a["L0_ffn_b1"].rearrange("(f p) -> p f", p=P),
                          allow_slow_non_contiguous=True).then_inc(cols_in, 16)

            act.wait_ge(kq_bias_in, 64)
            act.mul(kq_bias[:, 1, :], kq_bias[:, 1, :], SCALE).then_inc(bias_scaled, 1)
            act.wait_ge(bias_scaled, 1)

            def project_out(i):
                m, c, s = ITEMS[i]
                key = ("proj", i)
                src = is_filled(act, key)
                if i >= 2:
                    act.wait_ge(part_ready, i - 1)
                first = k_parts[:, c, 0, HALF * s:HALF * s + HALF] if m == K_ else q_parts[:, c, s, 0, :]
                scale = 1.0 if m == K_ else SCALE
                bias = kq_bias[:, 0 if m == K_ else 1, c:c + 1]
                act.activation(cut[:, i % 2, :], src, ACT.Identity, bias=bias, scale=scale)
                act.activation(first, src, ACT.Identity, bias=bias, scale=scale).then_inc(drain_sem(key), 1)

            for i in range(EARLY_ITEMS):
                project_out(i)
            for key in beside_max_pass():
                if key[0] == "proj":
                    project_out(key[1])
                if key[0] == "v":
                    src = is_filled(act, key)
                    act.copy(v_sb[:, key[1], :, :], src[:, 0:D].rearrange("p (h d) -> p h d", h=H)).then_inc(drain_sem(key), 1)
                    if key[1] == 1:
                        act.wait_ge(w1_in, 16)
                        act.wait_ge(w2_in, 16)
                        act.activation(pflat[:, 0:2048], w1_nat[:, :, :].rearrange("p f d -> p (f d)"), ACT.Abs,
                                       accum_out=abs_sum[:, 0:1]).then_inc(abs_ready, 1)
                        act.activation(pflat[:, 2048:4096], w2_nat[:, :, :].rearrange("p c f -> p (c f)"), ACT.Abs,
                                       accum_out=abs_sum[:, 1:2]).then_inc(abs_ready, 1)
            act.wait_ge(cols_in, 16)

            def copy_shift(u):
                act.wait_ge(filled[SHIFT_BANK], base[SHIFT_BANK] + u + 1)
                act.copy(m_rows[:, :], ps[:, SHIFT_BANK, 0:P // 2].bitcast(BF16)) \
                    .then_inc(drained[SHIFT_BANK], 1)

            def evacuate_pv(g, qh, u):
                act.wait_ge(filled[PV_BANK], base[PV_BANK] + u + 1)
                act.copy(o_un[:, bass.ds(g, 1), HALF * qh:HALF * qh + HALF].rearrange("p g t -> p (g t)"),
                         ps[:, PV_BANK, :]).then_inc(drained[PV_BANK], 1)

            def exp_tile(u, s):
                c, j = divmod(s, G)
                b = SCORE_BANKS[s % 2]
                act.wait_ge(filled[b], base[b] + u * (STEPS // 2) + (s // 2 + 1))
                if j == 0 and not (isinstance(u, int) and u == 0 and c < 2):
                    if c == 1:
                        act.wait_ge(filled[PV_BANK], base[PV_BANK] + u)
                    else:
                        act.wait_ge(pv_chunk, u * (TT - 1) + (c - 1 if c else 0))
                act.activation(pbuf[:, c % 2, j, :], ps[:, b, :], ACT.Exp).then_inc(drained[b], 1)

            def exp_unit(g, qh, u, more=True, last=False):
                for s in range(G, STEPS):
                    exp_tile(u, s)
                    if s == 27 and not last:
                        copy_shift(u + 1)
                if not last:
                    for s in range(G):
                        exp_tile(u + 1, s)
                evacuate_pv(g, qh, u)
                if more:
                    act.copy(v_slot[:, qh, :, :, 0:HD], v_sb[:, :, bass.ds((g + 1) * G, G), :]).then_inc(v_slot_ready, 1)

            for t in range(TT):
                is_drained(act, ("v", t))
            act.wait_ge(pads, 1)
            for qh in (0, 1):
                act.copy(v_slot[:, qh, :, :, 0:HD], v_sb[:, :, 0:G, :]).then_inc(v_slot_ready, 1)
            copy_shift(0)
            act.wait_ge(parts_out[4], 16)
            act.wait_ge(parts_out[5], 16)
            for s in range(G):
                exp_tile(0, s)
            with act.Fori(0, NG - 1) as g:
                exp_unit(g, 0, g * 2)
                exp_unit(g, 1, g * 2 + 1)
            exp_unit(NG - 1, 0, NU - 2, more=False)
            exp_unit(NG - 1, 1, NU - 1, more=False, last=True)

            def ternary_out(n):
                c = n // 2
                if n % 2 == 0:
                    key = ("w1t", c)
                    act.activation(w1T[:, c, :], is_filled(act, key).bitcast(BF16), ACT.Identity,
                                   scale=1.0 / X_SCALE).then_inc(drain_sem(key), 1)
                else:
                    key = ("w2t", c)
                    act.copy(w2T[:, 4 * c:4 * c + 4, :].rearrange("p f d -> p (f d)"),
                             is_filled(act, key).bitcast(BF16)).then_inc(drain_sem(key), 1)

            def o_out(key):
                act.copy(oT[:, number[key] % 2, :, :], is_filled(act, key)[:, 0:D].rearrange("p (c t) -> p c t", c=DC)) \
                    .then_inc(drain_sem(key), 1)

            def first_x_part(k, p):
                src = is_filled(act, ("lnt", k, p)).rearrange("p (c t) -> p c t", c=DC)
                act.mul(x12[:, 0, :, 256 * p:256 * p + 256], src, X_SCALE).then_inc(x1_ready, 1)

            def gelu(key):
                _, r, s, f = key
                src = is_filled(act, key)
                n = number[key]
                if n >= 4:
                    act.wait_ge(g3_ready, n - 3)
                act.activation(g_full[:, n % 4, :], src, ACT.Gelu, bias=b1_col[:, f:f + 1])
                act.activation(g_parts[:, 0, f, HALF * s:HALF * s + HALF], src, ACT.Gelu, bias=b1_col[:, f:f + 1]) \
                    .then_inc(drain_sem(key), 1)

            def gelu_second(r, s, f):
                n = number["g2", r, s, f]
                act.wait_ge(g_rest, n + 1)
                act.copy(g_parts[:, 1, f, HALF * s:HALF * s + HALF], g_full[:, n % 4, :]).then_inc(g2_ready, 1)

            def qkv_out(t):
                flat = qkv[t % 3].rearrange("p h n -> p (h n)")
                if t >= 3:
                    act.wait_ge(divided, t - 2)
                act.copy(flat[:, 0:512], is_filled(act, ("qk", t))).then_inc(drain_sem(("qk", t)), 1)
                act.copy(flat[:, 512:768], is_filled(act, ("kv", t))[:, 0:D]).then_inc(drain_sem(("kv", t)), 1)

            for e in events:
                if e[0] == "w":
                    ternary_out(e[1])
                if e[0] == "o":
                    o_out(e)
                if e[0] == "lnt":
                    (evacuate_lnt if e[1] == 2 else first_x_part)(*e[1:])
                if e[0] == "h":
                    gelu(e)
                if e[0] == "g2":
                    gelu_second(*e[1:])
                if e[0] == "qkv":
                    qkv_out(e[1])
                if e[0] == "soft":
                    t = e[1]
                    act.wait_ge(shifted, t + 1)
                    act.activation(probs[:, t % 2, :, :], probs[:, t % 2, :, :], ACT.Exp, scale=SCALE).then_inc(exped, 1)

        @block.vector
        def _(dve):
            steps = [0]

            def link(ins):
                steps[0] += 1
                ins.then_inc(dve_step, 1)
                dve.wait_ge(dve_step, steps[0])

            dve.memset(m_parts[:, :], 0.0)
            link(dve.memset(a_all[:, :, :, :].rearrange("p c m r -> p (c m r)"), 0.0))
            dve.memset(b_all[:, :], 0.0).then_inc(ab_padded, 1)

            def variances(k, p):
                if k == 0:
                    dve.wait_ge(x_in[p], 16)
                for t in (2 * p, 2 * p + 1):
                    dve.bn_stats(stats[:, t, :], x_res[:, t, :]).then_inc(dve_step, 1)
                    steps[0] += 1
                dve.wait_ge(dve_step, steps[0])
                for t in (2 * p, 2 * p + 1):
                    dve.bn_aggr(mv[:, t, :], stats[:, t, :]).then_inc(dve_step, 1)
                    steps[0] += 1
                dve.wait_ge(dve_step, steps[0])
                dve.tensor_scalar(rstd[:, 2 * p:2 * p + 2], mv[:, 2 * p:2 * p + 2, 1], EPS, None, ALU.add) \
                    .then_inc(stats_ready, 1)

            def normalise(k, p):
                n = number["norm", k, p]
                dve.wait_ge(rstd_ready, number["var", k, p] + 1)
                if n >= 2:
                    is_filled(dve, ("lnt", *norms[n - 2][1:]))
                for i in (0, 1):
                    t = 2 * p + i
                    ins = dve.tensor_scalar(xn[:, n % 2, i, :], x_res[:, t, :], mv[:, t, 0:1], rstd[:, t:t + 1],
                                            ALU.subtract, ALU.mult)
                ins.then_inc(xn_ready, 1)

            variances(0, 0)
            for p in range(PAIRS):
                if p + 1 < PAIRS:
                    variances(0, p + 1)
                normalise(0, p)

            def middle_part(i):
                m, c, s = ITEMS[i]
                v = slice(HALF * s, HALF * s + HALF)
                one = k_parts[:, c, 0, v] if m == K_ else q_parts[:, c, s, 0, :]
                two = k_parts[:, c, 1, v] if m == K_ else q_parts[:, c, s, 1, :]
                is_drained(dve, ("proj", i))
                link(dve.tensor_tensor(cut[:, i % 2, :], cut[:, i % 2, :], one, ALU.subtract))
                dve.tensor_copy(two, cut[:, i % 2, :]).then_inc(rest_ready, 1)

            for i in range(EARLY_ITEMS):
                middle_part(i)

            n_max = G * TT // 2

            def m_part(n):
                return m_parts[:, n_max * n:n_max * n + n_max]


            def take_max(u, k, par):
                b = PAIR_BANKS[k % 2]
                dve.wait_ge(filled[b], base[b] + u * (FILLS // 2) + (k // 2 + 1))
                dve.tensor_reduce(mx[:, par, k:k + 1], ps[:, b:b + 2, :].rearrange("p b k -> p (b k)"), AX_X, ALU.max) \
                    .then_inc(drained[b], 1)

            def cut_max(u, par):
                for b in PAIR_BANKS:
                    dve.wait_ge(drained[b], base[b] + u * (FILLS // 2) + FILLS // 2)
                dve.tensor_scalar(m_part(0), mx[:, par, :], -1.0, None, ALU.mult).then_inc(max_step, 1)
                dve.wait_ge(max_step, u * 3 + 1)
                dve.scalar_tensor_tensor(out=mrest[:, :], in0=mx[:, par, :], scalar=-1.0, in1=m_part(0),
                                         op0=ALU.mult, op1=ALU.subtract).then_inc(max_step, 1)
                dve.wait_ge(max_step, u * 3 + 2)
                dve.tensor_copy(m_part(1), mrest[:, :]).then_inc(max_step, 1)
                dve.wait_ge(max_step, u * 3 + 3)
                dve.tensor_tensor(m_part(2), mrest[:, :], m_part(1), ALU.subtract).then_inc(shift_split, 1)

            for k in range(FILLS):
                take_max(0, k, 0)
                if k in (2, 4):
                    middle_part(EARLY_ITEMS + (k - 2) // 2)
            cut_max(0, 0)
            for k in range(LEAD):
                take_max(1, k, 1)
            src = is_filled(dve, ("wsum",))
            dve.tensor_scalar(thr[:, :, 0], src[:, 0:2], 0.5 / (FF * D), 0.5 * WQ_EPS, ALU.mult, ALU.max)
            dve.tensor_scalar(thr[:, :, 1], src[:, 0:2], -0.5 / (FF * D), -0.5 * WQ_EPS, ALU.mult, ALU.min) \
                .then_inc(drain_sem(("wsum",)), 1)

            def unit_max(u, next_par):
                for k in range(LEAD, FILLS):
                    take_max(u + 1, k, next_par)
                cut_max(u + 1, next_par)

            def lead_max(u, par):
                for k in range(LEAD):
                    take_max(u, k, par)

            with dve.Fori(0, NG - 1) as g:
                unit_max(g * 2, 1)
                lead_max(g * 2 + 2, 0)
                unit_max(g * 2 + 1, 0)
                lead_max(g * 2 + 3, 1)
            unit_max(NU - 2, 1)

            def residual(r, t, key):
                dve.wait_ge(bias_added, 2 * number["norm", r, t // 2] + t % 2 + 1)
                src = is_filled(dve, key)
                dve.tensor_tensor(x_res[:, t, :], src[:, 0:D], x_res[:, t, :], ALU.add).then_inc(drain_sem(key), 1)
                if t % 2 == 1 and r < 3:
                    is_drained(dve, key)

            def divide(key):
                t = key[1]
                src = is_filled(dve, key).rearrange("p (h n) -> p h n", h=H)
                link(dve.reciprocal(rsum[:, t % 2, :], src[:, :, HD]))
                n = number["o", "a", t]
                if n >= 2:
                    is_filled(dve, outs[n - 2])
                dve.tensor_tensor(o_norm[:, n % 2, :].rearrange("p (h n) -> p h n", h=H), src[:, :, 0:HD],
                                  rsum[:, t % 2, :].unsqueeze(2).broadcast_to([P, H, HD]), ALU.mult) \
                    .then_inc(drain_sem(key), 1)

            def second_x_part(k, p):
                key = ("lnt", k, p)
                is_filled(dve, key)
                dve.wait_ge(x1_ready, x12_pairs.index(key) + 1)
                v = slice(256 * p, 256 * p + 256)
                dve.scalar_tensor_tensor(out=x12[:, 1, :, v], in0=bank(key).rearrange("p (c t) -> p c t", c=DC),
                                         scalar=X_SCALE, in1=x12[:, 0, :, v], op0=ALU.mult, op1=ALU.subtract) \
                    .then_inc(drain_sem(key), 1)

            def gelu_rest(r, s, f):
                is_drained(dve, ("h", r, s, f))
                g = g_full[:, number["g", r, s, f] % 4, :]
                dve.tensor_tensor(g, g, g_parts[:, 0, f, HALF * s:HALF * s + HALF], ALU.subtract).then_inc(g_rest, 1)

            taken = [0]

            def head_scores(t, quad):
                nj, i = 4 * quad + 4, slice(4 * quad, 4 * quad + 4)
                dst = s_raw[:, t % 2, i, 0:nj]
                if quad in POOL_QUADS:
                    slot = prod[:, taken[0] % 3, :]
                    taken[0] += 1
                    dve.wait_ge(products, taken[0])
                    _, _, terms = factors(t, quad, slot)
                    dve.tensor_reduce(dst, terms, AX_X, ALU.add).then_inc(reduced, 1)
                    return
                in0, in1, terms = factors(t, quad, prod_own[quad])
                link(dve.tensor_tensor(terms, in0, in1, ALU.mult))
                ins = dve.tensor_reduce(dst, terms, AX_X, ALU.add)
                if quad == 0:
                    link(ins)

            def soften(t):
                dve.wait_ge(reduced, taken[0])
                p = probs[:, t % 2, :, :]
                link(dve.tensor_tensor(p, s_raw[:, t % 2, :, :], causal[:, :, :], ALU.add))
                link(dve.tensor_reduce(hmax[:, :], p, AX_X, ALU.max))
                dve.tensor_tensor(p, p, hmax[:, :].unsqueeze(2).broadcast_to([P, H, H]), ALU.subtract).then_inc(shifted, 1)

            def head_outputs(t):
                w = probs[:, t % 2, :, :]
                dve.wait_ge(exped, t + 1)
                dve.tensor_reduce(v_sum[:, :], qkv[t % 3][:, :, 2 * HD:3 * HD].rearrange("p j d -> p d j"), AX_X, ALU.add)
                link(dve.tensor_reduce(hsum[:, :], w, AX_X, ALU.add))
                link(dve.reciprocal(hsum[:, :], hsum[:, :]))
                link(dve.tensor_tensor(w, w, hsum[:, :].unsqueeze(2).broadcast_to([P, H, H]), ALU.mult))
                link(dve.tensor_reduce(w_sum[:, :], w, AX_X, ALU.add))
                n = number["o", "b", t]
                is_filled(dve, outs[n - 2])
                dve.tensor_tensor(o_norm[:, n % 2, :].rearrange("p (h n) -> p h n", h=H),
                                  w_sum[:, :].unsqueeze(2).broadcast_to([P, H, HD]),
                                  v_sum[:, :].unsqueeze(1).broadcast_to([P, H, HD]), ALU.mult).then_inc(divided, 1)

            outs = [e for e in events if e[0] == "o"]
            x12_pairs = [e for e in events if e[0] == "lnt" and e[1] != 2]
            dve.wait_ge(pads, 2)
            dve.wait_ge(consts, 6)
            for e in events:
                if e[0] == "ao_t":
                    divide(e)
                if e[0] in ("ao_y", "bo_y"):
                    residual(0 if e[0] == "ao_y" else 2, e[1], e)
                if e[0] == "y":
                    residual(2 * e[1] + 1, e[2], e)
                if e[0] == "var":
                    variances(*e[1:])
                if e[0] == "norm":
                    normalise(*e[1:])
                if e[0] == "lnt" and e[1] != 2:
                    second_x_part(*e[1:])
                if e[0] == "g":
                    gelu_rest(*e[1:])
                if e[0] == "s":
                    if e[2] == QUADS - 1:
                        is_drained(dve, ("kv", e[1]))
                    head_scores(e[1], e[2])
                if e[0] == "soft":
                    soften(e[1])
                if e[0] == "div":
                    head_outputs(e[1])

        @block.tensor
        def _(pe):
            def lora_a_transposed(key):
                pe.wait_ge(consts, 2)
                pe.wait_ge(ab_in, 16 * 8)
                out = to_fill(pe, key)
                for c in range(DC):
                    ins = pe.transpose(out[:, P * c:P * c + P], a_all[:, c, :, :].rearrange("p m r -> p (m r)"), ident[:, :])
                ins.then_inc(fill_sem(key), 1)

            def merged_weight(key):
                m = key[1]
                if m == 0:
                    is_drained(pe, ("at",))
                pe.wait_ge(w_in[m], 16)
                out = to_fill(pe, key)
                r = slice(32 * m, 32 * m + RANK)
                for c in range(DC):
                    pe.matmul(out[:, D * c:D * c + D], b_all[r, P * c:P * c + P], aT[r, :], start=True, stop=False)
                    for o in range(DC):
                        ins = pe.matmul(out[:, D * c + P * o:D * c + P * o + P], w_nat[:, m, o, P * c:P * c + P],
                                        ident[:, :], start=False, stop=(o == DC - 1))
                ins.then_inc(fill_sem(key), 1)

            def transpose_pair(key):
                _, k, p = key
                n = number["norm", k, p]
                pe.wait_ge(xn_ready, n + 1)
                out = to_fill(pe, key)
                for c in range(DC):
                    for i in (0, 1):
                        ins = pe.transpose(out[:, 256 * c + P * i:256 * c + P * i + P], xn[:, n % 2, i, P * c:P * c + P],
                                           ident[:, :])
                ins.then_inc(fill_sem(key), 1)

            def project(key):
                m, c, s = ITEMS[key[1]]
                if key[1] == 0:
                    for i in range(4):
                        is_drained(pe, ("wt", i))
                for p in (2 * s, 2 * s + 1):
                    is_drained(pe, ("lnt", 0, p))
                out = to_fill(pe, key)
                for d in range(DC):
                    ins = pe.matmul(out, wT[:, m, d, P * c:P * c + P], xT[:, d, HALF * s:HALF * s + HALF],
                                    start=(d == 0), stop=(d == DC - 1))
                ins.then_inc(fill_sem(key), 1)

            def project_v(key):
                t = key[1]
                if t == 0:
                    pe.wait_ge(bv_in, 16)
                    pe.wait_ge(consts, 3)
                out = to_fill(pe, key)[:, 0:D]
                pe.matmul(out, ones[0:1, :], bv_row[:, :], start=True, stop=False)
                for d in range(DC):
                    ins = pe.matmul(out, xT[:, d, P * t:P * t + P], wT[:, V_, d, :], start=False, stop=(d == DC - 1))
                ins.then_inc(fill_sem(key), 1)

            def weight_sums(key):
                pe.wait_ge(abs_ready, 2)
                out = to_fill(pe, key)
                pe.matmul(out[:, 0:2], ones[:, :], abs_sum[:, :], start=True, stop=True).then_inc(fill_sem(key), 1)

            setup = {"at": lora_a_transposed, "wt": merged_weight, "lnt": transpose_pair, "proj": project,
                     "v": project_v, "wsum": weight_sums}
            for key in setup_order():
                setup[key[0]](key)

            def max_tile(g, qh, u, k):
                j, qt = divmod(k, TT // 2)
                b = PAIR_BANKS[k % 2]
                h = bass.ds(g * G + j, 1)
                if isinstance(u, int) and u == 0 and k < 2:
                    pass
                else:
                    pe.wait_ge(drained[b], base[b] + u * (FILLS // 2) + k // 2)
                for n in (0, 1):
                    ins = pe.matmul(ps[:, b + n, :], q_rows[0:ROWS, qh, h, P * qt:P * qt + P].rearrange("p h t -> p (h t)"),
                                    k_rows[0:ROWS, h, HALF * n:HALF * n + HALF].rearrange("p h t -> p (h t)"),
                                    start=True, stop=True)
                ins.then_inc(filled[b], 1)

            def shift_rows(u):
                pe.wait_ge(shift_split, u + 1)
                if isinstance(u, int) and u == 0:
                    if base[SHIFT_BANK]:
                        pe.wait_ge(drained[SHIFT_BANK], base[SHIFT_BANK])
                else:
                    pe.wait_ge(drained[SHIFT_BANK], base[SHIFT_BANK] + u)
                pe.transpose(ps[:, SHIFT_BANK, 0:P // 2].bitcast(BF16), m_parts[:, :], identb[:, :]).then_inc(filled[SHIFT_BANK], 1)

            def score_tile(g, qh, u, s):
                c, j = divmod(s, G)
                b = SCORE_BANKS[s % 2]
                pe.wait_ge(drained[b], base[b] + u * (STEPS // 2) + s // 2)
                h = bass.ds(g * G + j, 1)
                pe.matmul(ps[:, b, :], k_rows[0:SROWS, h, P * c:P * c + P].rearrange("p h t -> p (h t)"),
                          q_rows[0:SROWS, qh, h, :].rearrange("p h t -> p (h t)"), start=True, stop=True) \
                    .then_inc(filled[b], 1)

            def times_v(qh, u, c):
                for b in SCORE_BANKS:
                    pe.wait_ge(drained[b], base[b] + u * (STEPS // 2) + 2 * (c + 1))
                if c == 0:
                    pe.wait_ge(v_slot_ready, u + 1)
                    pe.wait_ge(drained[PV_BANK], base[PV_BANK] + u)
                for j in range(G):
                    ins = pe.matmul(ps[32 * j:32 * j + 32, PV_BANK, :], v_slot[:, qh, c, j, :], pbuf[:, c % 2, j, :],
                                    start=(c == 0), stop=(c == TT - 1))
                ins.then_inc(pv_chunk if c < TT - 1 else filled[PV_BANK], 1)

            pe.wait_ge(k_packed[0], 48)
            pe.wait_ge(q_packed[0], 48)
            side = beside_max_pass()
            for k in range(FILLS):
                max_tile(0, 0, 0, k)
                if side:
                    key = side.pop(0)
                    setup[key[0]](key)
            for key in side:
                setup[key[0]](key)
            pe.wait_ge(q_packed[1], 48)
            for k in range(LEAD):
                max_tile(0, 1, 1, k)
                if k == 1:
                    pe.wait_ge(consts, 5)
                    shift_rows(0)
            for s, n in ((k_packed[1], 48), (k_packed[2], 48), (q_packed[2], 48), (q_packed[3], 48), (q_packed[4], 48),
                         (ones_rows_in, 48)):
                pe.wait_ge(s, n)

            def unit(g, qh, u, nxt, after):
                fill = LEAD
                for s in range(2, STEPS + 2):
                    if s < STEPS:
                        score_tile(g, qh, u, s)
                    elif nxt is not None:
                        if s == STEPS:
                            pe.wait_ge(shift_landed, (u + 2) * 48)
                        score_tile(*nxt, s - STEPS)
                    if s % 2 == 1:
                        if fill < FILLS and nxt is not None:
                            max_tile(*nxt, fill)
                        elif fill >= FILLS and after is not None:
                            max_tile(*after, fill - FILLS)
                        fill += 1
                    if s == 26 and nxt is not None:
                        shift_rows(nxt[2])
                    if s % G == 1 and s > G:
                        times_v(qh, u, s // G - 1)

            pe.wait_ge(shift_landed, 48)
            score_tile(0, 0, 0, 0)
            score_tile(0, 0, 0, 1)
            with pe.Fori(0, NG - 1) as g:
                unit(g, 0, g * 2, (g, 1, g * 2 + 1), (g + 1, 0, g * 2 + 2))
                unit(g, 1, g * 2 + 1, (g + 1, 0, g * 2 + 2), (g + 1, 1, g * 2 + 3))
            unit(NG - 1, 0, NU - 2, (NG - 1, 1, NU - 1), None)
            unit(NG - 1, 1, NU - 1, None, None)

            def w1_transposed(key):
                c = key[1]
                if c == 0:
                    pe.wait_ge(tern_ready, 8)
                out = to_fill(pe, key).bitcast(BF16)
                for f in range(FC):
                    ins = pe.transpose(out[:, P * f:P * f + P], tern1[:, f, P * c:P * c + P], identb[:, :])
                ins.then_inc(fill_sem(key), 1)

            def w2_transposed(key):
                n = key[1]
                out = to_fill(pe, key).bitcast(BF16)
                for f in range(4):
                    for c in range(DC):
                        ins = pe.transpose(out[:, D * f + P * c:D * f + P * c + P],
                                           tern2[:, c, P * (4 * n + f):P * (4 * n + f) + P], identb[:, :])
                ins.then_inc(fill_sem(key), 1)

            def o_to_tokens(key):
                t = key[1]
                if t % 4 == 0:
                    pe.wait_ge(drained[PV_BANK], base[PV_BANK] + NU - 1 + t // 4)
                out = to_fill(pe, key)
                for g in range(NG):
                    ins = pe.transpose(out[:, P * g:P * g + P], o_un[:, g, P * t:P * t + P], ident[:, :])
                ins.then_inc(fill_sem(key), 1)

            def o_to_features(key):
                _, which, t = key
                n = number[key]
                if which == "a":
                    is_drained(pe, ("ao_t", t))
                else:
                    pe.wait_ge(divided, t + 1)
                out = to_fill(pe, key)
                for c in range(DC):
                    ins = pe.transpose(out[:, P * c:P * c + P], o_norm[:, n % 2, P * c:P * c + P], ident[:, :])
                ins.then_inc(fill_sem(key), 1)

            def project_o(key):
                which, t = ("a" if key[0] == "ao_y" else "b"), key[1]
                is_drained(pe, ("o", which, t))
                if which == "b" and t == 0:
                    pe.wait_ge(wout_in, 16)
                w = wT[:, O_, :, :] if which == "a" else w_out
                out = to_fill(pe, key)[:, 0:D]
                for c in range(DC):
                    ins = pe.matmul(out, oT[:, number["o", which, t] % 2, c, :], w[:, c, :], start=(c == 0),
                                    stop=(c == DC - 1))
                ins.then_inc(fill_sem(key), 1)

            def hidden(key):
                _, r, h, f = key
                k = 1 if r == 0 else 3
                if f == 0:
                    for p in (2 * h, 2 * h + 1):
                        is_drained(pe, ("lnt", k, p))
                    is_drained(pe, ("w1t", 1))
                out = to_fill(pe, key)
                for n in (0, 1):
                    for c in range(DC):
                        ins = pe.matmul(out, w1T[:, c, P * f:P * f + P], x12[:, n, c, HALF * h:HALF * h + HALF],
                                        start=(n == 0 and c == 0), stop=(n == 1 and c == DC - 1))
                ins.then_inc(fill_sem(key), 1)

            def ffn_out(key):
                _, r, t = key
                if t % 4 == 0:
                    pe.wait_ge(g3_ready, number["g2", r, t // 4, FC - 1] + 1)
                    is_drained(pe, ("w2t", 1))
                out = to_fill(pe, key)[:, 0:D]
                for f in range(FC):
                    for n in range(NPART):
                        ins = pe.matmul(out, g_parts[:, n, f, P * t:P * t + P], w2T[:, f, :],
                                        start=(f == 0 and n == 0), stop=(f == FC - 1 and n == NPART - 1))
                ins.then_inc(fill_sem(key), 1)

            def heads_qkv(key):
                t = key[1]
                cols = slice(0, 512) if key[0] == "qk" else slice(512, 768)
                is_drained(pe, ("lnt", 2, t // 2))
                if t == 0:
                    pe.wait_ge(wqkv_in, 32)
                out = to_fill(pe, key)[:, 0:cols.stop - cols.start]
                pe.matmul(out, ones[0:1, :], bqkv[:, cols], start=True, stop=False)
                for d in range(DC):
                    ins = pe.matmul(out, xT[:, d, P * t:P * t + P], wqkv[:, d, cols], start=False, stop=(d == DC - 1))
                ins.then_inc(fill_sem(key), 1)

            tail = {"w1t": w1_transposed, "w2t": w2_transposed, "ao_t": o_to_tokens, "o": o_to_features,
                    "ao_y": project_o, "lnt": transpose_pair, "h": hidden, "y": ffn_out, "qk": heads_qkv,
                    "kv": heads_qkv, "bo_y": project_o}
            for key in tail_order():
                tail[key[0]](key)


_INS = ["L0_attn_a_x", *[f"L0_attn_a_{w}{m}" for m in "qkvo" for w in "WbBA"], "L0_attn_b_Wqkv", "L0_attn_b_bqkv",
        "L0_attn_b_Wout", "L0_attn_b_bout", "L0_ffn_w1", "L0_ffn_b1", "L0_ffn_w2", "L0_ffn_b2"]


def kernel(**inputs):
    import numpy as _np
    import concourse.bacc as _bacc
    from concourse import mybir as _mybir
    from concourse.bass_utils import run_bass_kernel_spmd as _run

    nc = _bacc.Bacc("TRN2", target_bir_lowering=False, num_devices=1)
    arrays, aps = {}, {}
    for name in _INS:
        v = _np.ascontiguousarray(inputs[name])
        arrays[f"in_{name}_dram"] = v
        aps[name] = nc.dram_tensor(f"in_{name}_dram", v.shape, _mybir.dt.from_np(v.dtype), kind="ExternalInput").ap()
    aps["out"] = nc.dram_tensor("out_dram", (1, T, D), F32, kind="ExternalOutput").ap()
    build(nc, aps)
    r = _run(nc, [arrays], core_ids=[0])
    return r.results[0]["out_dram"]
```

```python
from contextlib import ExitStack

import concourse.bass as bass
from concourse import mybir

F32 = mybir.dt.float32
BF16 = mybir.dt.bfloat16
F16 = mybir.dt.float16
U32 = mybir.dt.uint32
ALU = mybir.AluOpType
ACT = mybir.ActivationFunctionType
AX_X = mybir.AxisListType.X

P = 128
T, D, H, HD, RANK, FF = 1024, 256, 16, 16, 16, 1024
TT = T // P
PAIRS = TT // 2
DC = D // P
FC = FF // P
HC = P // HD
G = 4
NG = H // G
HALF = T // 2
NU = NG * 2
NPART = 3
NTERM = 7
ROWS = NTERM * HD
SROWS = ROWS + NPART
STEPS = TT * G
SHIFT_AT = 23
RING_USES = (STEPS + 1) // 3
FILLS = G * TT // 2
LEAD = 7
LORA_SCALE = 8.0 / RANK
SCALE = HD ** -0.5
EPS = 1e-5
NEG = -1e9
WQ_EPS = 1e-8
X_SCALE = 2048.0
K_, Q_, V_, O_ = range(4)

PAIR_BANKS = (0, 2)
SCORE_BANKS = (4, 5, 7)
PV_BANK = 6
SETUP_BANKS = (4, 5, 7, 6)
BESIDE_LAST_UNIT = (0, 1, 2, 3)
TAIL_BANKS = (4, 5, 7, 6, 0, 1, 2, 3)

ITEMS = [(K_, 0, 0), (K_, 0, 1), (Q_, 0, 0), (Q_, 0, 1), (K_, 1, 0), (K_, 1, 1), (Q_, 1, 0), (Q_, 1, 1)]
EARLY_ITEMS = 6


def setup_order():
    yield ("at",)
    for m in range(4):
        yield ("wt", m)
        yield ("lnt", 0, m)
    for i in range(EARLY_ITEMS):
        yield ("proj", i)


def beside_max_pass():
    return [("proj", i) for i in range(EARLY_ITEMS, len(ITEMS))] + [("v", t) for t in range(TT)] + [("wsum",), ("shift",)]


QUADS = H // 4
POOL_QUADS = (3, 2)
LAST_STEP = 0.5
OUT_AT, OUT_STEP = (4.5, 18.0), 1.7
FFN_AT, H_STEP, Y_STEP = ((18.5, 42.0), (99.0, 131.0)), 1.7, 2.6
HEADS_AT, HEADS_STEP = (52.0, 84.0), 8.0


def pair_slots(k, p, at):
    if k < 4:
        yield at, ("var", k, p)
        yield at + 1.6, ("norm", k, p)
        yield at + 2.4, ("lnt", k, p)
        yield at + 2.8, ("lnt_out", k, p)
        if k != 2:
            yield at + 3.4, ("x_rest", k, p)


def last_unit_slots():
    for s in range(2, STEPS):
        yield LAST_STEP * s, ("score", s)
    for s in range(G, STEPS):
        yield LAST_STEP * s + 0.3, ("exp", s)
    for c in range(TT):
        yield LAST_STEP * (G * c + 5) + 0.2, ("pv", c)
    yield LAST_STEP * (STEPS + 1) + 1.2, ("pv_out",)


def output_slots(s):
    for i in range(4):
        t, at = 4 * s + i, OUT_AT[s] + OUT_STEP * i
        yield at, ("ao_t", t)
        yield at + 0.5, ("div", t)
        yield at + 1.6, ("o", "a", t)
        yield at + 1.9, ("o_out", "a", t)
        yield at + 2.5, ("ao_y", t)
        yield at + 3.4, ("res", 0, t)
        if t % 2:
            yield from pair_slots(1, t // 2, at + 3.5)


def ffn_slots(r, s):
    for f in range(FC):
        at = FFN_AT[r][s] + H_STEP * f
        for n, kind in enumerate(("h", "gelu", "g_rest", "g2", "g3")):
            yield at + (0.0, 0.9, 2.1, 2.8, 3.4)[n], (kind, r, s, f)
    for i in range(4):
        t, at = 4 * s + i, FFN_AT[r][s] + H_STEP * FC + 3.5 + Y_STEP * i
        yield at, ("y", r, t)
        yield at + 2.7, ("res", 2 * r + 1, t)
        if t % 2:
            yield from pair_slots(2 * r + 2, t // 2, at + 2.8)


def heads_slots(s):
    for i in range(4):
        t, at = 4 * s + i, HEADS_AT[s] + HEADS_STEP * i
        yield at, ("qk", t)
        yield at + 2.6, ("kv", t)
        yield at + 2.7, ("qk_out", t)
        yield at + 4.0, ("kv_out", t)
        for n in range(QUADS):
            quad = QUADS - 1 - n
            yield at + 4.6 + 2.0 * n, ("prod", t, quad)
            yield at + 6.9 + (0.0, 2.0, 3.0, 4.3)[n], ("sum", t, quad)
        yield at + 12.2, ("soft", t)
        yield at + 13.5, ("exp_heads", t)
        yield at + 14.0, ("wv", t)
        yield at + 16.3, ("o", "b", t)
        yield at + 16.7, ("o_out", "b", t)
        yield at + 17.2, ("bo_y", t)
        yield at + 18.2, ("res", 2, t)
        if t % 2:
            yield from pair_slots(3, t // 2, at + 18.3)


def tail_events():
    slots = [*last_unit_slots(), *((2.0 + n, ("w", n)) for n in range(4))]
    for s in (0, 1):
        slots += [*output_slots(s), *ffn_slots(0, s), *heads_slots(s), *ffn_slots(1, s)]
    return [event for _, event in sorted(slots, key=lambda slot: slot[0])]


TAIL_FILLS = ("w", "ao_t", "o", "ao_y", "lnt", "h", "y", "qk", "kv", "bo_y")


def numbered():
    of, count = {}, {}
    events = [(kind, 0, p) for kind in ("var", "norm", "lnt") for p in range(PAIRS)]
    for e in [*events, *tail_events()]:
        of[e] = count.get(e[0], 0)
        count[e[0]] = of[e] + 1
    return of


def ring_place(s, last):
    return s + (s >= SHIFT_AT and not last)


def ring_fills(place, i):
    return (place - i) // len(SCORE_BANKS) + 1


class Banks:

    def __init__(self):
        self.count = [0] * 8
        self.of = {}

    def claim(self, key, bank):
        self.of[key] = (bank, self.count[bank])
        self.count[bank] += 1


def plan_banks():
    banks = Banks()
    for n, key in enumerate([*setup_order(), *beside_max_pass()]):
        banks.claim(key, SETUP_BANKS[n % len(SETUP_BANKS)])
    base = list(banks.count)
    for b in PAIR_BANKS:
        banks.count[b] += NU * FILLS // 2
    for i, b in enumerate(SCORE_BANKS):
        banks.count[b] += (NU - 1) * RING_USES + ring_fills(STEPS - 1, i)
    banks.count[PV_BANK] += NU
    ring, n = BESIDE_LAST_UNIT, 0
    for e in tail_events():
        if e == ("pv", TT - 1):
            ring, n = TAIL_BANKS, 0
        if e[0] in TAIL_FILLS:
            banks.claim(e, ring[n % len(ring)])
            n += 1
    return banks.of, base


def build(nc, a):
    uses, base = plan_banks()
    number = numbered()
    events = list(tail_events())
    norms = [e for e in number if e[0] == "norm"]
    kparts_dram = nc.dram_tensor("k_parts", [NPART, DC, P, T], BF16, kind="Internal").ap()
    qparts_dram = nc.dram_tensor("q_parts", [NPART, 2, DC, P, HALF], BF16, kind="Internal").ap()

    with ExitStack() as ctx:
        def sb(name, shape, dt=F32):
            return ctx.enter_context(nc.sbuf_tensor(name, shape, dt))

        def sem(name):
            return ctx.enter_context(nc.semaphore(name))

        x_res = sb("x_res", [P, TT, D])
        xn = sb("xn", [P, 2, 2, D])
        xT = sb("xT", [P, DC, T])
        w_nat = sb("w_nat", [P, 4, DC, D])
        wT = sb("wT", [P, 4, DC, D])
        a_all = sb("a_all", [P, DC, 4, 32])
        b_all = sb("b_all", [P, D])
        aT = sb("aT", [P, D])
        cut = sb("cut", [P, 2, HALF])
        parts = sb("parts", [P, 12 * 1024], BF16)
        k_parts = parts[:, 0:6144].rearrange("p (c a t) -> p c a t", c=DC, a=NPART)
        q_parts = parts[:, 6144:12288].rearrange("p (c h a t) -> p c h a t", c=DC, h=2, a=NPART)
        o_un = parts[:, 0:8192].bitcast(F32).rearrange("p (g t) -> p g t", g=NG)
        pack = sb("pack", [P, 32 * 1024], BF16)
        k_rows = pack[:, 0:16384].rearrange("p (h t) -> p h t", h=H)
        q_rows = pack[:, 16384:32768].rearrange("p (s h t) -> p s h t", s=2, h=H)
        k_group = pack[:, 0:16384].rearrange("p (g j t) -> p g j t", g=NG, j=G)
        q_group = pack[:, 16384:32768].rearrange("p (s g j t) -> p s g j t", s=2, g=NG, j=G)
        g_parts = pack[:, 0:24576].rearrange("p (a f t) -> p a f t", a=NPART, f=FC)
        g_full = pack[:, 24576:28672].bitcast(F32).rearrange("p (r t) -> p r t", r=4)
        qkv_rooms = wT[:, 0:3, :, :].rearrange("p m c d -> p (m c d)")
        qkv = [room.rearrange("p (h n) -> p h n", h=H)
               for room in (qkv_rooms[:, 0:768], qkv_rooms[:, 768:1536],
                            cut[:, :, :].rearrange("p a t -> p (a t)")[:, 0:768])]
        v_sb = sb("v_sb", [P, TT, H, HD])
        x12 = v_sb[:, :, :, :].rearrange("p t h d -> p (t h d)").bitcast(F16).rearrange("p (n c t) -> p n c t", n=2, c=DC)
        v_slot = sb("v_slot", [P, 2, TT, G, 32])
        pbuf = sb("pbuf", [P, 2, G, HALF])
        pflat = pbuf[:, :, :, :].rearrange("p a g t -> p (a g t)")
        prod = pflat[:, 0:3072].rearrange("p (r n) -> p r n", r=3)
        prod_own = {1: pflat[:, 3072:3584], 0: pflat[:, 3584:3840]}
        late = parts[:, 8192:12288].bitcast(F32)
        o_norm = late[:, 0:512].rearrange("p (r n) -> p r n", r=2)
        oT = late[:, 512:1024].rearrange("p (r c t) -> p r c t", r=2, c=DC)
        probs = late[:, 1024:1536].rearrange("p (r i j) -> p r i j", r=2, i=H)
        s_raw = sb("s_raw", [P, 2, H, H])
        w_out = sb("w_out", [P, DC, D])
        wqkv = w_nat[:, 0:3, :, :].rearrange("p m c d -> p (m c d)").rearrange("p (c n) -> p c n", c=DC)
        bqkv = sb("bqkv", [1, H * 3 * HD])
        w1_nat = sb("w1_nat", [P, FC, D])
        w2_nat = sb("w2_nat", [P, DC, FF])
        w1T = w1_nat[:, 0:4, :].rearrange("p f d -> p (f d)").bitcast(F16).rearrange("p (c f) -> p c f", c=DC)
        w2T = w2_nat[:, 0:1, :].rearrange("p c f -> p (c f)").bitcast(BF16).rearrange("p (f d) -> p f d", f=FC)
        tern1 = sb("tern1", [P, FC, D], BF16)
        tern2 = sb("tern2", [P, DC, FF], BF16)
        below = sb("below", [P, 512], BF16)
        above = sb("above", [P, 512], BF16)
        ident = sb("ident", [P, P])
        identb = sb("identb", [P, P], BF16)
        ones = sb("ones", [P, P])
        onesb = sb("onesb", [P, HALF], BF16)
        causal = sb("causal", [P, H, H])
        kq_bias = sb("kq_bias", [P, 2, DC])
        b1_col = sb("b1_col", [P, FC])
        rows = sb("rows", [P, 3, D])
        bv_row = sb("bv_row", [1, D])
        stats = sb("stats", [P, TT, 6])
        mv = sb("mv", [P, TT, 2])
        rstd = sb("rstd", [P, TT])
        minus_half = sb("minus_half", [P, 2])
        abs_sum = sb("abs_sum", [P, 2])
        thr = sb("thr", [P, 2, 2])
        mx = sb("mx", [P, 2, G * TT // 2])
        mrest = sb("mrest", [P, G * TT // 2])
        m_parts = sb("m_parts", [P, P], BF16)
        m_rows = sb("m_rows", [P, P], BF16)
        rsum = sb("rsum", [P, 2, H])
        hmax = sb("hmax", [P, H])
        hsum = sb("hsum", [P, H])
        w_sum = sb("w_sum", [P, H])
        v_sum = sb("v_sum", [P, HD])

        ps = ctx.enter_context(nc.psum_tensor("ps", [P, 8, 512], F32))

        filled = [sem(f"filled{b}") for b in range(8)]
        drained = [sem(f"drained{b}") for b in range(8)]
        x_in = [sem(f"x_in{p}") for p in range(PAIRS)]
        w_in = [sem(f"w_in{m}") for m in range(4)]
        ab_padded = sem("ab_padded")
        ab_in = sem("ab_in")
        bias_scaled = sem("bias_scaled")
        wout_in = sem("wout_in")
        pv_chunk = sem("pv_chunk")
        kq_bias_in = sem("kq_bias_in")
        bv_in = sem("bv_in")
        rows_in = sem("rows_in")
        cols_in = sem("cols_in")
        w1_in = sem("w1_in")
        w2_in = sem("w2_in")
        wqkv_in = sem("wqkv_in")
        ones_rows_in = sem("ones_rows_in")
        consts = sem("consts")
        pads = sem("pads")
        stats_ready = sem("stats_ready")
        rstd_ready = sem("rstd_ready")
        xn_ready = sem("xn_ready")
        bias_added = sem("bias_added")
        rest_ready = sem("rest_ready")
        part_ready = sem("part_ready")
        parts_out = [sem(f"parts_out{i}") for i in range(6)]
        k_packed = [sem(f"k_packed{i}") for i in range(3)]
        q_packed = [sem(f"q_packed{i}") for i in range(5)]
        dve_step = sem("dve_step")
        pool_step = sem("pool_step")
        max_step = sem("max_step")
        shift_split = sem("shift_split")
        shift_landed = sem("shift_landed")
        v_slot_ready = sem("v_slot_ready")
        abs_ready = sem("abs_ready")
        tern_ready = sem("tern_ready")
        x1_ready = sem("x1_ready")
        g_rest = sem("g_rest")
        g2_ready = sem("g2_ready")
        g3_ready = sem("g3_ready")
        products = sem("products")
        reduced = sem("reduced")
        shifted = sem("shifted")
        exped = sem("exped")
        divided = sem("divided")
        stored = sem("stored")

        def bank(key):
            return ps[:, uses[key][0], :]

        def to_fill(pe, key):
            b, n = uses[key]
            if n:
                pe.wait_ge(drained[b], n)
            return ps[:, b, :]

        def is_filled(eng, key):
            b, n = uses[key]
            eng.wait_ge(filled[b], n + 1)
            return ps[:, b, :]

        def is_drained(eng, key):
            b, n = uses[key]
            eng.wait_ge(drained[b], n + 1)

        def fill_sem(key):
            return filled[uses[key][0]]

        def drain_sem(key):
            return drained[uses[key][0]]

        def factors(t, quad, out):
            nj, i = 4 * quad + 4, slice(4 * quad, 4 * quad + 4)
            shape = [P, 4, nj, HD]
            in0 = qkv[t % 3][:, i, 0:HD].unsqueeze(2).broadcast_to(shape)
            in1 = qkv[t % 3][:, 0:nj, HD:2 * HD].unsqueeze(1).broadcast_to(shape)
            return in0, in1, out[:, 0:4 * nj * HD].rearrange("p (i j n) -> p i j n", i=4, j=nj)

        block = ctx.enter_context(nc.Block())

        @block.sync
        def _(sp):
            xv = a["L0_attn_a_x"].rearrange("o (t p) d -> (o p) t d", p=P)
            for p in range(PAIRS):
                sp.dma_start(x_res[:, 2 * p:2 * p + 2, :], xv[:, 2 * p:2 * p + 2, :]).then_inc(x_in[p], 16)
            for m, name in ((V_, "Wv"), (O_, "Wo")):
                sp.dma_start(w_nat[:, m, :, :],
                             a[f"L0_attn_a_{name}"].rearrange("(c p) d -> p c d", p=P)).then_inc(w_in[m], 16)
            sp.dma_start(bv_row[:, :], a["L0_attn_a_bv"].rearrange("(a n) -> a n", a=1)).then_inc(bv_in, 16)
            for n, name in enumerate(("L0_attn_a_bo", "L0_ffn_b2", "L0_attn_b_bout")):
                sp.dma_start(rows[:, n, :], bass.AP(a[name].tensor, 0, [[0, P], [1, D]])).then_inc(rows_in, 16)
            sp.dma_start(bqkv[:, :], a["L0_attn_b_bqkv"].rearrange("(a h) n -> a (h n)", a=1)).then_inc(wqkv_in, 16)
            sp.dma_start(w_out[:, :, :], a["L0_attn_b_Wout"].rearrange("h d m -> (h d) m")
                         .rearrange("(c p) m -> p c m", p=P)).then_inc(wout_in, 16)
            sp.wait_ge(consts, 4)
            for j in range(NPART):
                sp.dma_start(k_rows[ROWS + j:ROWS + j + 1, :, :].rearrange("o h t -> o (h t)"),
                             onesb[0:H * T // HALF, :]).then_inc(ones_rows_in, 16)

            def store_k(n, c):
                sp.wait_ge(part_ready, 2 if c == 0 else 6)
                sp.dma_start(kparts_dram[:, c, :, :].rearrange("a f t -> f a t"), k_parts[:, c, :, :]) \
                    .then_inc(parts_out[n], 16)

            def store_q(n, c, s):
                sp.wait_ge(part_ready, ITEMS.index((Q_, c, s)) + 1)
                sp.dma_start(qparts_dram[:, s, c, :, :].rearrange("a f t -> f a t"), q_parts[:, c, s, :, :]) \
                    .then_inc(parts_out[n], 16)

            def pack_k(n, c, h0, nh, done):
                sp.wait_ge(parts_out[n], 16)
                at = kparts_dram[0:1, c:c + 1, :, :].offset + h0 * T
                for row, first, count in ((0, 0, 3), (3, 0, 3), (6, 0, 1)):
                    src = bass.AP(kparts_dram.tensor, at + first * DC * P * T,
                                  [[DC * P * T, count], [HC * T, HD], [1, nh * T]])
                    sp.dma_start(k_rows[row * HD:(row + count) * HD, HC * c + h0:HC * c + h0 + nh, :]
                                 .rearrange("p h t -> p (h t)"), src).then_inc(done, 16)

            def pack_q(n, c, s, h0, nh, done):
                sp.wait_ge(parts_out[n], 16)
                at = qparts_dram[0:1, s:s + 1, c:c + 1, :, :].offset + h0 * HALF
                for row, part, count in ((0, 0, 3), (3, 1, 3), (6, 2, 1)):
                    src = bass.AP(qparts_dram.tensor, at + part * 2 * DC * P * HALF,
                                  [[0, count], [HC * HALF, HD], [1, nh * HALF]])
                    sp.dma_start(q_rows[row * HD:(row + count) * HD, s, HC * c + h0:HC * c + h0 + nh, :]
                                 .rearrange("p h t -> p (h t)"), src).then_inc(done, 16)

            store_k(0, 0)
            pack_k(0, 0, 0, G, k_packed[0])
            store_q(1, 0, 0)
            pack_q(1, 0, 0, 0, G, q_packed[0])
            store_q(2, 0, 1)
            pack_q(2, 0, 1, 0, HC, q_packed[1])
            pack_k(0, 0, G, G, k_packed[1])
            pack_q(1, 0, 0, G, G, q_packed[2])
            store_k(3, 1)
            pack_k(3, 1, 0, HC, k_packed[2])
            store_q(4, 1, 0)
            pack_q(4, 1, 0, 0, HC, q_packed[3])
            store_q(5, 1, 1)
            pack_q(5, 1, 1, 0, HC, q_packed[4])

            def land_shift(g, qh, u):
                if isinstance(u, int) and u == 0:
                    is_drained(sp, ("shift",))
                else:
                    i = SHIFT_AT % len(SCORE_BANKS)
                    b = SCORE_BANKS[i]
                    sp.wait_ge(drained[b], u * RING_USES + (base[b] + ring_fills(SHIFT_AT, i) - RING_USES))
                n = G * TT // 2
                for j in range(NPART):
                    sp.dma_start(q_rows[ROWS + j:ROWS + j + 1, qh, bass.ds(g * G, G), :]
                                 .rearrange("o h t -> o (h t)"), m_rows[n * j:n * j + n, :]) \
                        .then_inc(shift_landed, 16)

            land_shift(0, 0, 0)
            with sp.Fori(0, NG - 1) as g:
                land_shift(g, 1, g * 2 + 1)
                land_shift(g + 1, 0, g * 2 + 2)
            land_shift(NG - 1, 1, NU - 1)

            ov = a["out"].rearrange("o (t p) d -> (o p) t d", p=P)
            for p in range(PAIRS):
                for t in (2 * p, 2 * p + 1):
                    is_drained(sp, ("y", 1, t))
                sp.dma_start(ov[:, 2 * p:2 * p + 2, :], x_res[:, 2 * p:2 * p + 2, :]).then_inc(stored, 16)
            sp.wait_ge(stored, 16 * PAIRS)

        @block.gpsimd
        def _(pool):
            steps = [0]

            def link(ins):
                steps[0] += 1
                ins.then_inc(pool_step, 1)
                pool.wait_ge(pool_step, steps[0])

            def eye(t):
                link(pool.memset(t[:, :], 0.0))
                pool.affine_select(out=t[:, :], in_=t[:, :], compare_op=ALU.not_equal, fill=1.0, base=0,
                                   pattern=[[-1, P]], channel_multiplier=1).then_inc(consts, 1)

            pool.memset(minus_half[:, :], -0.5).then_inc(consts, 1)
            eye(ident)
            pool.memset(ones[:, :], 1.0).then_inc(consts, 1)
            pool.memset(onesb[:, :], 1.0).then_inc(consts, 1)
            eye(identb)

            pool.wait_ge(consts, 5)

            def inverse_deviations(k, p):
                pool.wait_ge(stats_ready, number["var", k, p] + 1)
                pool.tensor_tensor(rstd[:, 2 * p:2 * p + 2], rstd[:, 2 * p:2 * p + 2], minus_half[:, :], ALU.pow) \
                    .then_inc(rstd_ready, 1)

            def add_bias(r, p):
                pool.wait_ge(xn_ready, number["norm", r, p] + 1)
                if r == 0 and p == 0:
                    pool.wait_ge(rows_in, 48)
                row = (0, 1, 2, 1)[r]
                for t in (2 * p, 2 * p + 1):
                    pool.tensor_tensor(x_res[:, t, :], x_res[:, t, :], rows[:, row, :], ALU.add).then_inc(bias_added, 1)

            for p in range(PAIRS):
                inverse_deviations(0, p)

            def third_part(i):
                m, c, s = ITEMS[i]
                dst = k_parts[:, c, 2, HALF * s:HALF * s + HALF] if m == K_ else q_parts[:, c, s, 2, :]
                mid = k_parts[:, c, 1, HALF * s:HALF * s + HALF] if m == K_ else q_parts[:, c, s, 1, :]
                pool.wait_ge(rest_ready, i + 1)
                pool.tensor_tensor(dst, cut[:, i % 2, :], mid, ALU.subtract).then_inc(part_ready, 1)

            for i in range(EARLY_ITEMS):
                third_part(i)
            pool.memset(v_slot[:, :, :, :, HD:32], 1.0).then_inc(pads, 1)
            for i in range(EARLY_ITEMS, len(ITEMS)):
                third_part(i)
            pool.memset(s_raw[:, :, :, :], 0.0).then_inc(pads, 1)
            link(pool.memset(causal[:, :, :], 0.0))
            pool.affine_select(out=causal[:, :, :], in_=causal[:, :, :], compare_op=ALU.is_ge, fill=NEG, base=0,
                               pattern=[[1, H], [-1, H]], channel_multiplier=0).then_inc(consts, 1)
            for p in range(PAIRS):
                add_bias(0, p)


            is_drained(pool, ("wsum",))
            for n, (w, tern) in enumerate(((w1_nat, tern1), (w2_nat, tern2))):
                wf = w[:, :, :].rearrange("p c d -> p (c d)")
                tf = tern[:, :, :].rearrange("p c d -> p (c d)")
                for c in range(4):
                    v = slice(512 * c, 512 * c + 512)
                    link(pool.tensor_scalar(below[:, :], wf[:, v], thr[:, n, 1:2], None, ALU.is_lt))
                    link(pool.tensor_scalar(above[:, :], wf[:, v], thr[:, n, 0:1], None, ALU.is_gt))
                    pool.tensor_tensor(tf[:, v], above[:, :], below[:, :], ALU.subtract).then_inc(tern_ready, 1)
                    pool.wait_ge(tern_ready, 4 * n + c + 1)

            def third_gelu_part(r, s, f):
                n = number["h", r, s, f]
                pool.wait_ge(g2_ready, n + 1)
                v = slice(HALF * s, HALF * s + HALF)
                pool.tensor_tensor(g_parts[:, 2, f, v], g_full[:, n % 4, :], g_parts[:, 1, f, v], ALU.subtract) \
                    .then_inc(g3_ready, 1)

            made = [0]

            def product(t, quad):
                if quad == QUADS - 1:
                    is_drained(pool, ("kv", t))
                if made[0] >= 3:
                    pool.wait_ge(reduced, made[0] - 2)
                in0, in1, out = factors(t, quad, prod[:, made[0] % 3, :])
                pool.tensor_tensor(out, in0, in1, ALU.mult).then_inc(products, 1)
                made[0] += 1

            for e in events:
                if e[0] == "var":
                    inverse_deviations(*e[1:])
                if e[0] == "norm":
                    add_bias(*e[1:])
                if e[0] == "g3":
                    third_gelu_part(*e[1:])
                if e[0] == "prod" and e[2] in POOL_QUADS:
                    product(e[1], e[2])

        @block.scalar
        def _(act):
            for m, name in ((K_, "Wk"), (Q_, "Wq")):
                act.dma_start(w_nat[:, m, :, :],
                              a[f"L0_attn_a_{name}"].rearrange("(c p) d -> p c d", p=P)).then_inc(w_in[m], 16)
            act.wait_ge(ab_padded, 1)
            for m, n in ((K_, "k"), (Q_, "q"), (V_, "v"), (O_, "o")):
                act.dma_start(a_all[:, :, m, 0:RANK], a[f"L0_attn_a_A{n}"].rearrange("(c p) r -> p c r", p=P)) \
                    .then_inc(ab_in, 16)
                act.dma_start(b_all[32 * m:32 * m + RANK, :], a[f"L0_attn_a_B{n}"]).then_inc(ab_in, 16)
            for n, name in enumerate(("bk", "bq")):
                t = a[f"L0_attn_a_{name}"].tensor
                for c in range(DC):
                    act.dma_start(kq_bias[:, n, c:c + 1], bass.AP(t, P * c, [[1, HD], [HD, HC], [1, 1]]),
                                  allow_slow_non_contiguous=True) \
                        .then_inc(kq_bias_in, 16)
            act.dma_start(w1_nat[:, :, :], a["L0_ffn_w1"].rearrange("(f p) d -> p f d", p=P)).then_inc(w1_in, 16)
            act.dma_start(w2_nat[:, :, :], a["L0_ffn_w2"].rearrange("(c p) f -> p c f", p=P)).then_inc(w2_in, 16)

            is_filled(act, ("at",))
            act.mul(aT[:, :], bank(("at",))[:, 0:D], LORA_SCALE).then_inc(drain_sem(("at",)), 1)

            def evacuate_lnt(k, p):
                src = is_filled(act, ("lnt", k, p)).rearrange("p (c t) -> p c t", c=DC)
                act.copy(xT[:, :, 256 * p:256 * p + 256], src).then_inc(drain_sem(("lnt", k, p)), 1)

            for m in range(4):
                key = ("wt", m)
                src = is_filled(act, key)
                if m in (K_, Q_):
                    for c in range(DC):
                        ins = act.copy(wT[:, m, c, :].rearrange("p (f d h) -> p f d h", f=DC, d=HD),
                                       src[:, D * c:D * c + D].rearrange("p (f h d) -> p f d h", f=DC, h=HC))
                else:
                    ins = act.copy(wT[:, m, :, :], src.rearrange("p (c n) -> p c n", c=DC))
                ins.then_inc(drain_sem(key), 1)
                evacuate_lnt(0, m)
            act.dma_start(wqkv[:, :, :], a["L0_attn_b_Wqkv"].rearrange("(c p) h n -> p c (h n)", p=P)).then_inc(wqkv_in, 16)
            act.dma_start(b1_col[:, :], a["L0_ffn_b1"].rearrange("(f p) -> p f", p=P),
                          allow_slow_non_contiguous=True).then_inc(cols_in, 16)

            act.wait_ge(kq_bias_in, 64)
            act.mul(kq_bias[:, 1, :], kq_bias[:, 1, :], SCALE).then_inc(bias_scaled, 1)
            act.wait_ge(bias_scaled, 1)

            def project_out(i):
                m, c, s = ITEMS[i]
                key = ("proj", i)
                src = is_filled(act, key)
                if i >= 2:
                    act.wait_ge(part_ready, i - 1)
                first = k_parts[:, c, 0, HALF * s:HALF * s + HALF] if m == K_ else q_parts[:, c, s, 0, :]
                scale = 1.0 if m == K_ else SCALE
                bias = kq_bias[:, 0 if m == K_ else 1, c:c + 1]
                act.activation(cut[:, i % 2, :], src, ACT.Identity, bias=bias, scale=scale)
                act.activation(first, src, ACT.Identity, bias=bias, scale=scale).then_inc(drain_sem(key), 1)

            for i in range(EARLY_ITEMS):
                project_out(i)
            for key in beside_max_pass():
                if key[0] == "proj":
                    project_out(key[1])
                if key[0] == "v":
                    src = is_filled(act, key)
                    act.copy(v_sb[:, key[1], :, :], src[:, 0:D].rearrange("p (h d) -> p h d", h=H)).then_inc(drain_sem(key), 1)
                    if key[1] == 1:
                        act.wait_ge(w1_in, 16)
                        act.wait_ge(w2_in, 16)
                        act.activation(pflat[:, 0:2048], w1_nat[:, :, :].rearrange("p f d -> p (f d)"), ACT.Abs,
                                       accum_out=abs_sum[:, 0:1]).then_inc(abs_ready, 1)
                        act.activation(pflat[:, 2048:4096], w2_nat[:, :, :].rearrange("p c f -> p (c f)"), ACT.Abs,
                                       accum_out=abs_sum[:, 1:2]).then_inc(abs_ready, 1)
            act.wait_ge(cols_in, 16)

            def copy_shift(u):
                if isinstance(u, int) and u == 0:
                    key = ("shift",)
                    src = is_filled(act, key)[:, 0:P // 2].bitcast(BF16)
                    act.copy(m_rows[:, :], src).then_inc(drain_sem(key), 1)
                    return
                i = SHIFT_AT % len(SCORE_BANKS)
                b = SCORE_BANKS[i]
                act.wait_ge(filled[b], u * RING_USES + (base[b] + ring_fills(SHIFT_AT, i) - RING_USES))
                act.copy(m_rows[:, :], ps[:, b, 0:P // 2].bitcast(BF16)).then_inc(drained[b], 1)

            def evacuate_pv(g, qh, u):
                act.wait_ge(filled[PV_BANK], base[PV_BANK] + u + 1)
                act.copy(o_un[:, bass.ds(g, 1), HALF * qh:HALF * qh + HALF].rearrange("p g t -> p (g t)"),
                         ps[:, PV_BANK, :]).then_inc(drained[PV_BANK], 1)

            def exp_tile(u, s):
                c, j = divmod(s, G)
                place = ring_place(s, isinstance(u, int) and u == NU - 1)
                i = place % len(SCORE_BANKS)
                b = SCORE_BANKS[i]
                act.wait_ge(filled[b], base[b] + u * RING_USES + ring_fills(place, i))
                if j == 0 and not (isinstance(u, int) and u == 0 and c < 2):
                    if c == 1:
                        act.wait_ge(filled[PV_BANK], base[PV_BANK] + u)
                    else:
                        act.wait_ge(pv_chunk, u * (TT - 1) + (c - 1 if c else 0))
                act.activation(pbuf[:, c % 2, j, :], ps[:, b, :], ACT.Exp).then_inc(drained[b], 1)

            def exp_unit(g, qh, u, more=True):
                for s in range(G, STEPS):
                    if s == SHIFT_AT:
                        copy_shift(u + 1)
                    exp_tile(u, s)
                for s in range(G):
                    exp_tile(u + 1, s)
                evacuate_pv(g, qh, u)
                if more:
                    act.copy(v_slot[:, qh, :, :, 0:HD], v_sb[:, :, bass.ds((g + 1) * G, G), :]).then_inc(v_slot_ready, 1)

            for t in range(TT):
                is_drained(act, ("v", t))
            act.wait_ge(pads, 1)
            for qh in (0, 1):
                act.copy(v_slot[:, qh, :, :, 0:HD], v_sb[:, :, 0:G, :]).then_inc(v_slot_ready, 1)
            copy_shift(0)
            act.wait_ge(parts_out[4], 16)
            act.wait_ge(parts_out[5], 16)
            for s in range(G):
                exp_tile(0, s)
            with act.Fori(0, NG - 1) as g:
                exp_unit(g, 0, g * 2)
                exp_unit(g, 1, g * 2 + 1)
            exp_unit(NG - 1, 0, NU - 2, more=False)

            def ternary_out(n):
                c, key = n // 2, ("w", n)
                if n % 2 == 0:
                    act.activation(w1T[:, c, :], is_filled(act, key).bitcast(BF16), ACT.Identity,
                                   scale=1.0 / X_SCALE).then_inc(drain_sem(key), 1)
                else:
                    act.copy(w2T[:, 4 * c:4 * c + 4, :].rearrange("p f d -> p (f d)"),
                             is_filled(act, key).bitcast(BF16)).then_inc(drain_sem(key), 1)

            def o_out(key):
                act.copy(oT[:, number[key] % 2, :, :], is_filled(act, key)[:, 0:D].rearrange("p (c t) -> p c t", c=DC)) \
                    .then_inc(drain_sem(key), 1)

            def first_x_part(k, p):
                src = is_filled(act, ("lnt", k, p)).rearrange("p (c t) -> p c t", c=DC)
                act.mul(x12[:, 0, :, 256 * p:256 * p + 256], src, X_SCALE).then_inc(x1_ready, 1)

            def gelu(key):
                _, r, s, f = key
                src = is_filled(act, key)
                n = number[key]
                if n >= 4:
                    act.wait_ge(g3_ready, n - 3)
                act.activation(g_full[:, n % 4, :], src, ACT.Gelu, bias=b1_col[:, f:f + 1])
                act.activation(g_parts[:, 0, f, HALF * s:HALF * s + HALF], src, ACT.Gelu, bias=b1_col[:, f:f + 1]) \
                    .then_inc(drain_sem(key), 1)

            def gelu_second(r, s, f):
                n = number["h", r, s, f]
                act.wait_ge(g_rest, n + 1)
                act.copy(g_parts[:, 1, f, HALF * s:HALF * s + HALF], g_full[:, n % 4, :]).then_inc(g2_ready, 1)

            def qk_out(t):
                if t >= 3:
                    act.wait_ge(divided, t - 2)
                act.copy(qkv[t % 3].rearrange("p h n -> p (h n)")[:, 0:512], is_filled(act, ("qk", t))) \
                    .then_inc(drain_sem(("qk", t)), 1)

            def kv_out(t):
                act.copy(qkv[t % 3].rearrange("p h n -> p (h n)")[:, 512:768], is_filled(act, ("kv", t))[:, 0:D]) \
                    .then_inc(drain_sem(("kv", t)), 1)

            def exp_heads(t):
                act.wait_ge(shifted, t + 1)
                act.activation(probs[:, t % 2, :, :], probs[:, t % 2, :, :], ACT.Exp, scale=SCALE).then_inc(exped, 1)

            for e in events:
                if e[0] == "exp":
                    exp_tile(NU - 1, e[1])
                if e[0] == "pv_out":
                    evacuate_pv(NG - 1, 1, NU - 1)
                if e[0] == "w":
                    ternary_out(e[1])
                if e[0] == "o_out":
                    o_out(("o", *e[1:]))
                if e[0] == "lnt_out":
                    (evacuate_lnt if e[1] == 2 else first_x_part)(*e[1:])
                if e[0] == "gelu":
                    gelu(("h", *e[1:]))
                if e[0] == "g2":
                    gelu_second(*e[1:])
                if e[0] == "qk_out":
                    qk_out(e[1])
                if e[0] == "kv_out":
                    kv_out(e[1])
                if e[0] == "exp_heads":
                    exp_heads(e[1])

        @block.vector
        def _(dve):
            steps = [0]

            def link(ins):
                steps[0] += 1
                ins.then_inc(dve_step, 1)
                dve.wait_ge(dve_step, steps[0])

            dve.memset(m_parts[:, :], 0.0)
            link(dve.memset(a_all[:, :, :, :].rearrange("p c m r -> p (c m r)"), 0.0))
            dve.memset(b_all[:, :], 0.0).then_inc(ab_padded, 1)

            def variances(k, p):
                if k == 0:
                    dve.wait_ge(x_in[p], 16)
                for t in (2 * p, 2 * p + 1):
                    dve.bn_stats(stats[:, t, :], x_res[:, t, :]).then_inc(dve_step, 1)
                    steps[0] += 1
                dve.wait_ge(dve_step, steps[0])
                for t in (2 * p, 2 * p + 1):
                    dve.bn_aggr(mv[:, t, :], stats[:, t, :]).then_inc(dve_step, 1)
                    steps[0] += 1
                dve.wait_ge(dve_step, steps[0])
                dve.tensor_scalar(rstd[:, 2 * p:2 * p + 2], mv[:, 2 * p:2 * p + 2, 1], EPS, None, ALU.add) \
                    .then_inc(stats_ready, 1)

            def normalise(k, p):
                n = number["norm", k, p]
                dve.wait_ge(rstd_ready, number["var", k, p] + 1)
                if n >= 2:
                    is_filled(dve, ("lnt", *norms[n - 2][1:]))
                for i in (0, 1):
                    t = 2 * p + i
                    ins = dve.tensor_scalar(xn[:, n % 2, i, :], x_res[:, t, :], mv[:, t, 0:1], rstd[:, t:t + 1],
                                            ALU.subtract, ALU.mult)
                ins.then_inc(xn_ready, 1)

            variances(0, 0)
            for p in range(PAIRS):
                if p + 1 < PAIRS:
                    variances(0, p + 1)
                normalise(0, p)

            def middle_part(i):
                m, c, s = ITEMS[i]
                v = slice(HALF * s, HALF * s + HALF)
                one = k_parts[:, c, 0, v] if m == K_ else q_parts[:, c, s, 0, :]
                two = k_parts[:, c, 1, v] if m == K_ else q_parts[:, c, s, 1, :]
                is_drained(dve, ("proj", i))
                link(dve.tensor_tensor(cut[:, i % 2, :], cut[:, i % 2, :], one, ALU.subtract))
                dve.tensor_copy(two, cut[:, i % 2, :]).then_inc(rest_ready, 1)

            for i in range(EARLY_ITEMS):
                middle_part(i)

            n_max = G * TT // 2

            def m_part(n):
                return m_parts[:, n_max * n:n_max * n + n_max]


            def take_max(u, k, par):
                b = PAIR_BANKS[k % 2]
                dve.wait_ge(filled[b], base[b] + u * (FILLS // 2) + (k // 2 + 1))
                dve.tensor_reduce(mx[:, par, k:k + 1], ps[:, b:b + 2, :].rearrange("p b k -> p (b k)"), AX_X, ALU.max) \
                    .then_inc(drained[b], 1)

            def cut_max(u, par):
                for b in PAIR_BANKS:
                    dve.wait_ge(drained[b], base[b] + u * (FILLS // 2) + FILLS // 2)
                dve.tensor_scalar(m_part(0), mx[:, par, :], -1.0, None, ALU.mult).then_inc(max_step, 1)
                dve.wait_ge(max_step, u * 3 + 1)
                dve.scalar_tensor_tensor(out=mrest[:, :], in0=mx[:, par, :], scalar=-1.0, in1=m_part(0),
                                         op0=ALU.mult, op1=ALU.subtract).then_inc(max_step, 1)
                dve.wait_ge(max_step, u * 3 + 2)
                dve.tensor_copy(m_part(1), mrest[:, :]).then_inc(max_step, 1)
                dve.wait_ge(max_step, u * 3 + 3)
                dve.tensor_tensor(m_part(2), mrest[:, :], m_part(1), ALU.subtract).then_inc(shift_split, 1)

            for k in range(FILLS):
                take_max(0, k, 0)
                if k in (2, 4):
                    middle_part(EARLY_ITEMS + (k - 2) // 2)
            cut_max(0, 0)
            for k in range(LEAD):
                take_max(1, k, 1)
            src = is_filled(dve, ("wsum",))
            dve.tensor_scalar(thr[:, :, 0], src[:, 0:2], 0.5 / (FF * D), 0.5 * WQ_EPS, ALU.mult, ALU.max)
            dve.tensor_scalar(thr[:, :, 1], src[:, 0:2], -0.5 / (FF * D), -0.5 * WQ_EPS, ALU.mult, ALU.min) \
                .then_inc(drain_sem(("wsum",)), 1)

            def unit_max(u, next_par):
                for k in range(LEAD, FILLS):
                    take_max(u + 1, k, next_par)
                cut_max(u + 1, next_par)

            def lead_max(u, par):
                for k in range(LEAD):
                    take_max(u, k, par)

            with dve.Fori(0, NG - 1) as g:
                unit_max(g * 2, 1)
                lead_max(g * 2 + 2, 0)
                unit_max(g * 2 + 1, 0)
                lead_max(g * 2 + 3, 1)
            unit_max(NU - 2, 1)

            def residual(r, t, key):
                dve.wait_ge(bias_added, 2 * number["norm", r, t // 2] + t % 2 + 1)
                src = is_filled(dve, key)
                dve.tensor_tensor(x_res[:, t, :], src[:, 0:D], x_res[:, t, :], ALU.add).then_inc(drain_sem(key), 1)
                if t % 2 == 1 and r < 3:
                    is_drained(dve, key)

            def divide(key):
                t = key[1]
                src = is_filled(dve, key).rearrange("p (h n) -> p h n", h=H)
                link(dve.reciprocal(rsum[:, t % 2, :], src[:, :, HD]))
                n = number["o", "a", t]
                if n >= 2:
                    is_filled(dve, outs[n - 2])
                dve.tensor_tensor(o_norm[:, n % 2, :].rearrange("p (h n) -> p h n", h=H), src[:, :, 0:HD],
                                  rsum[:, t % 2, :].unsqueeze(2).broadcast_to([P, H, HD]), ALU.mult) \
                    .then_inc(drain_sem(key), 1)

            def second_x_part(k, p):
                key = ("lnt", k, p)
                is_filled(dve, key)
                dve.wait_ge(x1_ready, x12_pairs.index(key) + 1)
                v = slice(256 * p, 256 * p + 256)
                dve.scalar_tensor_tensor(out=x12[:, 1, :, v], in0=bank(key).rearrange("p (c t) -> p c t", c=DC),
                                         scalar=X_SCALE, in1=x12[:, 0, :, v], op0=ALU.mult, op1=ALU.subtract) \
                    .then_inc(drain_sem(key), 1)

            def gelu_rest(r, s, f):
                is_drained(dve, ("h", r, s, f))
                g = g_full[:, number["h", r, s, f] % 4, :]
                dve.tensor_tensor(g, g, g_parts[:, 0, f, HALF * s:HALF * s + HALF], ALU.subtract).then_inc(g_rest, 1)

            taken = [0]

            def head_scores(t, quad):
                if quad == QUADS - 1:
                    is_drained(dve, ("kv", t))
                nj, i = 4 * quad + 4, slice(4 * quad, 4 * quad + 4)
                dst = s_raw[:, t % 2, i, 0:nj]
                if quad in POOL_QUADS:
                    slot = prod[:, taken[0] % 3, :]
                    taken[0] += 1
                    dve.wait_ge(products, taken[0])
                    _, _, terms = factors(t, quad, slot)
                    dve.tensor_reduce(dst, terms, AX_X, ALU.add).then_inc(reduced, 1)
                    return
                in0, in1, terms = factors(t, quad, prod_own[quad])
                link(dve.tensor_tensor(terms, in0, in1, ALU.mult))
                ins = dve.tensor_reduce(dst, terms, AX_X, ALU.add)
                if quad == 0:
                    link(ins)

            def soften(t):
                dve.wait_ge(reduced, taken[0])
                p = probs[:, t % 2, :, :]
                link(dve.tensor_tensor(p, s_raw[:, t % 2, :, :], causal[:, :, :], ALU.add))
                link(dve.tensor_reduce(hmax[:, :], p, AX_X, ALU.max))
                dve.tensor_tensor(p, p, hmax[:, :].unsqueeze(2).broadcast_to([P, H, H]), ALU.subtract).then_inc(shifted, 1)

            def head_outputs(t):
                w = probs[:, t % 2, :, :]
                dve.wait_ge(exped, t + 1)
                dve.tensor_reduce(v_sum[:, :], qkv[t % 3][:, :, 2 * HD:3 * HD].rearrange("p j d -> p d j"), AX_X, ALU.add)
                link(dve.tensor_reduce(hsum[:, :], w, AX_X, ALU.add))
                link(dve.reciprocal(hsum[:, :], hsum[:, :]))
                link(dve.tensor_tensor(w, w, hsum[:, :].unsqueeze(2).broadcast_to([P, H, H]), ALU.mult))
                link(dve.tensor_reduce(w_sum[:, :], w, AX_X, ALU.add))
                n = number["o", "b", t]
                is_filled(dve, outs[n - 2])
                dve.tensor_tensor(o_norm[:, n % 2, :].rearrange("p (h n) -> p h n", h=H),
                                  w_sum[:, :].unsqueeze(2).broadcast_to([P, H, HD]),
                                  v_sum[:, :].unsqueeze(1).broadcast_to([P, H, HD]), ALU.mult).then_inc(divided, 1)

            outs = [e for e in events if e[0] == "o"]
            x12_pairs = [e for e in events if e[0] == "lnt" and e[1] != 2]
            dve.wait_ge(pads, 2)
            dve.wait_ge(consts, 6)
            for e in events:
                if e[0] == "div":
                    divide(("ao_t", e[1]))
                if e[0] == "res":
                    r, t = e[1:]
                    residual(r, t, (("ao_y", t), ("y", 0, t), ("bo_y", t), ("y", 1, t))[r])
                if e[0] == "var":
                    variances(*e[1:])
                if e[0] == "norm":
                    normalise(*e[1:])
                if e[0] == "x_rest":
                    second_x_part(*e[1:])
                if e[0] == "g_rest":
                    gelu_rest(*e[1:])
                if e[0] == "sum":
                    head_scores(e[1], e[2])
                if e[0] == "soft":
                    soften(e[1])
                if e[0] == "wv":
                    head_outputs(e[1])

        @block.tensor
        def _(pe):
            def lora_a_transposed(key):
                pe.wait_ge(consts, 2)
                pe.wait_ge(ab_in, 16 * 8)
                out = to_fill(pe, key)
                for c in range(DC):
                    ins = pe.transpose(out[:, P * c:P * c + P], a_all[:, c, :, :].rearrange("p m r -> p (m r)"), ident[:, :])
                ins.then_inc(fill_sem(key), 1)

            def merged_weight(key):
                m = key[1]
                if m == 0:
                    is_drained(pe, ("at",))
                pe.wait_ge(w_in[m], 16)
                out = to_fill(pe, key)
                r = slice(32 * m, 32 * m + RANK)
                for c in range(DC):
                    pe.matmul(out[:, D * c:D * c + D], b_all[r, P * c:P * c + P], aT[r, :], start=True, stop=False)
                    for o in range(DC):
                        ins = pe.matmul(out[:, D * c + P * o:D * c + P * o + P], w_nat[:, m, o, P * c:P * c + P],
                                        ident[:, :], start=False, stop=(o == DC - 1))
                ins.then_inc(fill_sem(key), 1)

            def transpose_pair(key):
                _, k, p = key
                n = number["norm", k, p]
                pe.wait_ge(xn_ready, n + 1)
                out = to_fill(pe, key)
                for c in range(DC):
                    for i in (0, 1):
                        ins = pe.transpose(out[:, 256 * c + P * i:256 * c + P * i + P], xn[:, n % 2, i, P * c:P * c + P],
                                           ident[:, :])
                ins.then_inc(fill_sem(key), 1)

            def project(key):
                m, c, s = ITEMS[key[1]]
                if key[1] == 0:
                    for i in range(4):
                        is_drained(pe, ("wt", i))
                for p in (2 * s, 2 * s + 1):
                    is_drained(pe, ("lnt", 0, p))
                out = to_fill(pe, key)
                for d in range(DC):
                    ins = pe.matmul(out, wT[:, m, d, P * c:P * c + P], xT[:, d, HALF * s:HALF * s + HALF],
                                    start=(d == 0), stop=(d == DC - 1))
                ins.then_inc(fill_sem(key), 1)

            def project_v(key):
                t = key[1]
                if t == 0:
                    pe.wait_ge(bv_in, 16)
                    pe.wait_ge(consts, 3)
                out = to_fill(pe, key)[:, 0:D]
                pe.matmul(out, ones[0:1, :], bv_row[:, :], start=True, stop=False)
                for d in range(DC):
                    ins = pe.matmul(out, xT[:, d, P * t:P * t + P], wT[:, V_, d, :], start=False, stop=(d == DC - 1))
                ins.then_inc(fill_sem(key), 1)

            def weight_sums(key):
                pe.wait_ge(abs_ready, 2)
                out = to_fill(pe, key)
                pe.matmul(out[:, 0:2], ones[:, :], abs_sum[:, :], start=True, stop=True).then_inc(fill_sem(key), 1)

            setup = {"at": lora_a_transposed, "wt": merged_weight, "lnt": transpose_pair, "proj": project,
                     "v": project_v, "wsum": weight_sums}
            for key in setup_order():
                setup[key[0]](key)

            def max_tile(g, qh, u, k):
                j, qt = divmod(k, TT // 2)
                b = PAIR_BANKS[k % 2]
                at = bass.ds(g, 1)
                if isinstance(u, int) and u == 0 and k < 2:
                    pass
                else:
                    pe.wait_ge(drained[b], base[b] + u * (FILLS // 2) + k // 2)
                for n in (0, 1):
                    ins = pe.matmul(ps[:, b + n, :], q_group[0:ROWS, qh, at, j, P * qt:P * qt + P].rearrange("p g t -> p (g t)"),
                                    k_group[0:ROWS, at, j, HALF * n:HALF * n + HALF].rearrange("p g t -> p (g t)"),
                                    start=True, stop=True)
                ins.then_inc(filled[b], 1)

            def shift_rows(u):
                pe.wait_ge(shift_split, u + 1)
                if isinstance(u, int) and u == 0:
                    b = uses["shift",][0]
                    to_fill(pe, ("shift",))
                else:
                    i = SHIFT_AT % len(SCORE_BANKS)
                    b = SCORE_BANKS[i]
                    pe.wait_ge(drained[b], u * RING_USES + (base[b] + ring_fills(SHIFT_AT, i) - RING_USES - 1))
                pe.transpose(ps[:, b, 0:P // 2].bitcast(BF16), m_parts[:, :], identb[:, :]).then_inc(filled[b], 1)

            def score_tile(g, qh, u, s):
                c, j = divmod(s, G)
                place = ring_place(s, isinstance(u, int) and u == NU - 1)
                i = place % len(SCORE_BANKS)
                b = SCORE_BANKS[i]
                pe.wait_ge(drained[b], base[b] + u * RING_USES + (ring_fills(place, i) - 1))
                at = bass.ds(g, 1)
                pe.matmul(ps[:, b, :], k_group[0:SROWS, at, j, P * c:P * c + P].rearrange("p g t -> p (g t)"),
                          q_group[0:SROWS, qh, at, j, :].rearrange("p g t -> p (g t)"), start=True, stop=True) \
                    .then_inc(filled[b], 1)

            def times_v(qh, u, c):
                place = ring_place(G * c + G - 1, isinstance(u, int) and u == NU - 1)
                i = place % len(SCORE_BANKS)
                b = SCORE_BANKS[i]
                pe.wait_ge(drained[b], base[b] + u * RING_USES + ring_fills(place, i))
                if c == 0:
                    pe.wait_ge(v_slot_ready, u + 1)
                    pe.wait_ge(drained[PV_BANK], base[PV_BANK] + u)
                for j in range(G):
                    ins = pe.matmul(ps[32 * j:32 * j + 32, PV_BANK, :], v_slot[:, qh, c, j, :], pbuf[:, c % 2, j, :],
                                    start=(c == 0), stop=(c == TT - 1))
                ins.then_inc(pv_chunk if c < TT - 1 else filled[PV_BANK], 1)

            pe.wait_ge(k_packed[0], 48)
            pe.wait_ge(q_packed[0], 48)
            side = [key for key in beside_max_pass() if key[0] != "shift"]
            for k in range(FILLS):
                max_tile(0, 0, 0, k)
                if side:
                    key = side.pop(0)
                    setup[key[0]](key)
            for key in side:
                setup[key[0]](key)
            pe.wait_ge(q_packed[1], 48)
            for k in range(LEAD):
                max_tile(0, 1, 1, k)
                if k == 1:
                    pe.wait_ge(consts, 5)
                    shift_rows(0)
            for s, n in ((k_packed[1], 48), (k_packed[2], 48), (q_packed[2], 48), (q_packed[3], 48), (q_packed[4], 48),
                         (ones_rows_in, 48)):
                pe.wait_ge(s, n)

            def unit(g, qh, u, nxt, after):
                fill = LEAD
                for s in range(2, STEPS + 2):
                    if s == SHIFT_AT and nxt is not None:
                        shift_rows(nxt[2])
                    if s < STEPS:
                        score_tile(g, qh, u, s)
                    elif nxt is not None:
                        if s == STEPS:
                            pe.wait_ge(shift_landed, (u + 2) * 48)
                        score_tile(*nxt, s - STEPS)
                    if s % 2 == 1:
                        if fill < FILLS and nxt is not None:
                            max_tile(*nxt, fill)
                        elif fill >= FILLS and after is not None:
                            max_tile(*after, fill - FILLS)
                        fill += 1
                    if s % G == 1 and s > G:
                        times_v(qh, u, s // G - 1)

            pe.wait_ge(shift_landed, 48)
            score_tile(0, 0, 0, 0)
            score_tile(0, 0, 0, 1)
            with pe.Fori(0, NG - 1) as g:
                unit(g, 0, g * 2, (g, 1, g * 2 + 1), (g + 1, 0, g * 2 + 2))
                unit(g, 1, g * 2 + 1, (g + 1, 0, g * 2 + 2), (g + 1, 1, g * 2 + 3))
            unit(NG - 1, 0, NU - 2, (NG - 1, 1, NU - 1), None)
            def w_transposed(key):
                n, second = divmod(key[1], 2)
                if key[1] == 0:
                    pe.wait_ge(tern_ready, 8)
                (w2_transposed if second else w1_transposed)(key, n)

            def w1_transposed(key, c):
                out = to_fill(pe, key).bitcast(BF16)
                for f in range(FC):
                    ins = pe.transpose(out[:, P * f:P * f + P], tern1[:, f, P * c:P * c + P], identb[:, :])
                ins.then_inc(fill_sem(key), 1)

            def w2_transposed(key, n):
                out = to_fill(pe, key).bitcast(BF16)
                for f in range(4):
                    for c in range(DC):
                        ins = pe.transpose(out[:, D * f + P * c:D * f + P * c + P],
                                           tern2[:, c, P * (4 * n + f):P * (4 * n + f) + P], identb[:, :])
                ins.then_inc(fill_sem(key), 1)

            def o_to_tokens(key):
                t = key[1]
                if t % 4 == 0:
                    pe.wait_ge(drained[PV_BANK], base[PV_BANK] + NU - 1 + t // 4)
                out = to_fill(pe, key)
                for g in range(NG):
                    ins = pe.transpose(out[:, P * g:P * g + P], o_un[:, g, P * t:P * t + P], ident[:, :])
                ins.then_inc(fill_sem(key), 1)

            def o_to_features(key):
                _, which, t = key
                n = number[key]
                if which == "a":
                    is_drained(pe, ("ao_t", t))
                else:
                    pe.wait_ge(divided, t + 1)
                out = to_fill(pe, key)
                for c in range(DC):
                    ins = pe.transpose(out[:, P * c:P * c + P], o_norm[:, n % 2, P * c:P * c + P], ident[:, :])
                ins.then_inc(fill_sem(key), 1)

            def project_o(key):
                which, t = ("a" if key[0] == "ao_y" else "b"), key[1]
                is_drained(pe, ("o", which, t))
                if which == "b" and t == 0:
                    pe.wait_ge(wout_in, 16)
                w = wT[:, O_, :, :] if which == "a" else w_out
                out = to_fill(pe, key)[:, 0:D]
                for c in range(DC):
                    ins = pe.matmul(out, oT[:, number["o", which, t] % 2, c, :], w[:, c, :], start=(c == 0),
                                    stop=(c == DC - 1))
                ins.then_inc(fill_sem(key), 1)

            def hidden(key):
                _, r, h, f = key
                k = 1 if r == 0 else 3
                if f == 0:
                    for p in (2 * h, 2 * h + 1):
                        is_drained(pe, ("lnt", k, p))
                    is_drained(pe, ("w", 2))
                out = to_fill(pe, key)
                for n in (0, 1):
                    for c in range(DC):
                        ins = pe.matmul(out, w1T[:, c, P * f:P * f + P], x12[:, n, c, HALF * h:HALF * h + HALF],
                                        start=(n == 0 and c == 0), stop=(n == 1 and c == DC - 1))
                ins.then_inc(fill_sem(key), 1)

            def ffn_out(key):
                _, r, t = key
                if t % 4 == 0:
                    pe.wait_ge(g3_ready, number["h", r, t // 4, FC - 1] + 1)
                    is_drained(pe, ("w", 3))
                out = to_fill(pe, key)[:, 0:D]
                for f in range(FC):
                    for n in range(NPART):
                        ins = pe.matmul(out, g_parts[:, n, f, P * t:P * t + P], w2T[:, f, :],
                                        start=(f == 0 and n == 0), stop=(f == FC - 1 and n == NPART - 1))
                ins.then_inc(fill_sem(key), 1)

            def heads_qkv(key):
                t = key[1]
                cols = slice(0, 512) if key[0] == "qk" else slice(512, 768)
                is_drained(pe, ("lnt", 2, t // 2))
                if t == 0:
                    pe.wait_ge(wqkv_in, 32)
                out = to_fill(pe, key)[:, 0:cols.stop - cols.start]
                pe.matmul(out, ones[0:1, :], bqkv[:, cols], start=True, stop=False)
                for d in range(DC):
                    ins = pe.matmul(out, xT[:, d, P * t:P * t + P], wqkv[:, d, cols], start=False, stop=(d == DC - 1))
                ins.then_inc(fill_sem(key), 1)

            tail = {"w": w_transposed, "ao_t": o_to_tokens, "o": o_to_features, "ao_y": project_o,
                    "lnt": transpose_pair, "h": hidden, "y": ffn_out, "qk": heads_qkv, "kv": heads_qkv,
                    "bo_y": project_o}
            for e in events:
                if e[0] == "score":
                    score_tile(NG - 1, 1, NU - 1, e[1])
                if e[0] == "pv":
                    times_v(1, NU - 1, e[1])
                if e[0] in TAIL_FILLS:
                    tail[e[0]](e)


_INS = ["L0_attn_a_x", *[f"L0_attn_a_{w}{m}" for m in "qkvo" for w in "WbBA"], "L0_attn_b_Wqkv", "L0_attn_b_bqkv",
        "L0_attn_b_Wout", "L0_attn_b_bout", "L0_ffn_w1", "L0_ffn_b1", "L0_ffn_w2", "L0_ffn_b2"]


def kernel(**inputs):
    import numpy as _np
    import concourse.bacc as _bacc
    from concourse import mybir as _mybir
    from concourse.bass_utils import run_bass_kernel_spmd as _run

    nc = _bacc.Bacc("TRN2", target_bir_lowering=False, num_devices=1)
    arrays, aps = {}, {}
    for name in _INS:
        v = _np.ascontiguousarray(inputs[name])
        arrays[f"in_{name}_dram"] = v
        aps[name] = nc.dram_tensor(f"in_{name}_dram", v.shape, _mybir.dt.from_np(v.dtype), kind="ExternalInput").ap()
    aps["out"] = nc.dram_tensor("out_dram", (1, T, D), F32, kind="ExternalOutput").ap()
    build(nc, aps)
    r = _run(nc, [arrays], core_ids=[0])
    return r.results[0]["out_dram"]
```

```python
from contextlib import ExitStack

import concourse.bass as bass
from concourse import mybir

F32 = mybir.dt.float32
BF16 = mybir.dt.bfloat16
F16 = mybir.dt.float16
U32 = mybir.dt.uint32
ALU = mybir.AluOpType
ACT = mybir.ActivationFunctionType
AX_X = mybir.AxisListType.X

P = 128
T, D, H, HD, RANK, FF = 1024, 256, 16, 16, 16, 1024
TT = T // P
PAIRS = TT // 2
DC = D // P
FC = FF // P
HC = P // HD
G = 4
NG = H // G
HALF = T // 2
NU = NG * 2
NPART = 3
NTERM = 7
ROWS = NTERM * HD
SROWS = ROWS + NPART
STEPS = TT * G
SHIFT_AT = 23
RING_USES = (STEPS + 1) // 3
FILLS = G * TT // 2
LEAD = 7
LORA_SCALE = 8.0 / RANK
SCALE = HD ** -0.5
EPS = 1e-5
NEG = -1e9
WQ_EPS = 1e-8
X_SCALE = 2048.0
K_, Q_, V_, O_ = range(4)

BIAS_AT = {"qk": 0, "bo": 512, "b2": 768, "bout": 1024, "bv": 1280}
BIAS_COLS = 1536

PAIR_BANKS = (0, 2)
SCORE_BANKS = (4, 5, 7)
PV_BANK = 6
SETUP_BANKS = (4, 5, 7, 6)
BESIDE_LAST_UNIT = (0, 1, 2, 3)
TAIL_BANKS = (4, 5, 7, 6, 2, 3)
Y_BANKS = (0, 1)

ITEMS = [(K_, 0, 0), (K_, 0, 1), (Q_, 0, 0), (Q_, 0, 1), (K_, 1, 0), (K_, 1, 1), (Q_, 1, 0), (Q_, 1, 1)]


def setup_order():
    yield ("at",)
    yield ("lnt", 0, 0)
    yield ("lnt", 0, 1)
    yield ("wt", K_)
    yield ("lnt", 0, 2)
    yield ("wt", Q_)
    yield ("lnt", 0, 3)
    for i in range(len(ITEMS)):
        yield ("proj", i)
    yield ("wt", V_)
    yield ("wt", O_)


def beside_max_pass():
    return [("v", t) for t in range(TT)] + [("wsum",), ("shift",)]


QUADS = H // 4
LAST_STEP = 0.45
LAST_LAG = (0.3, 2.7, 17.8)
RANGES = (((0, 2), (2, 2), (4, 2), (6, 2)), ((0, 2), (2, 2), (4, 2), (6, 2)))
W_AT = 1.23
OUT_AT = (4.53, 21.4)
OUT_STEP = 1.65
OUT_LAG = (0.0, 0.59, 1.73, 1.87, 2.5, 3.39)
PAIR_LAG = (0.3, 2.08, 2.49, 2.9, 3.61)
FFN_AT = ((17.55, 26.0, 36.0, 46.0), (69.0, 87.48, 104.35, 119.18))
H_STEP = ((1.21, 1.21, 1.3, 1.31), (1.32, 1.27, 1.7, 1.21))
Y_STEP = 1.26
FFN_LAG = (-0.11, 1.6, 1.95, 2.92, 3.44, 5.0)
Y_LAG = 1.36
HEADS_AT = (39.0, 47.93, 56.72, 63.93, 72.93, 78.84, 81.69, 89.69)
HEADS_LAG = (0.0, 2.6, 2.7, 3.32, 9.89, 11.1, 11.36, 13.07, 13.77, 14.1, 15.1)
PROD_LAG = (3.4, 5.43, 7.0, 7.6)
SUM_LAG = 2.2
Y_LAST = FC - 2


def pair_slots(k, p, at):
    if k < 4:
        for lag, kind in zip(PAIR_LAG, ("var", "norm", "lnt", "lnt_out", "x_rest")):
            if kind != "x_rest" or k != 2:
                yield at + lag, (kind, k, p)


def last_unit_slots():
    exp_lag, pv_lag, out_at = LAST_LAG
    for s in range(2, STEPS):
        yield LAST_STEP * s, ("score", s)
    for s in range(G, STEPS):
        yield LAST_STEP * s + exp_lag, ("exp", s)
    for c in range(TT):
        yield LAST_STEP * G * c + pv_lag, ("pv", c)
    yield out_at, ("pv_out",)


def output_slots(s):
    for i in range(4):
        t, at = 4 * s + i, OUT_AT[s] + OUT_STEP * i
        for lag, event in zip(OUT_LAG, (("ao_t", t), ("div", t), ("o", "a", t), ("o_out", "a", t), ("ao_y", t),
                                        ("res", 0, t))):
            yield at + lag, event
        if t % 2:
            yield from pair_slots(1, t // 2, at + OUT_LAG[-1])


def range_of(r, t):
    return next(s for s, (first, n) in enumerate(RANGES[r]) if first <= t < first + n)


def ffn_slots(r, s):
    first, n = RANGES[r][s]
    h_step = H_STEP[r][s]
    for f in range(FC):
        at = FFN_AT[r][s] + h_step * f
        for lag, kind in zip(FFN_LAG, ("h", "gelu", "g_rest", "g2", "g3", "y_part")):
            if kind != "y_part" or f < Y_LAST:
                yield at + lag, (kind, r, s, f)
    for i in range(n // 2):
        p, at = first // 2 + i, FFN_AT[r][s] + h_step * (FC - 1) + FFN_LAG[-1] + Y_STEP * i
        yield at, ("y", r, p)
        yield at + Y_LAG, ("res_pair", r, p)
        yield from pair_slots(2 * r + 2, p, at + Y_LAG)


def heads_slots():
    for t, at in enumerate(HEADS_AT):
        for lag, event in zip(HEADS_LAG, (("qk", t), ("vs", t), ("qk_out", t), ("vs_out", t), ("soft", t),
                                          ("exp_heads", t), ("wv", t), ("o", "b", t), ("o_out", "b", t), ("bo_y", t),
                                          ("res", 2, t))):
            yield at + lag, event
        for n in range(QUADS):
            yield at + PROD_LAG[n], ("prod", t, QUADS - 1 - n)
            yield at + PROD_LAG[n] + SUM_LAG, ("sum", t, QUADS - 1 - n)
        if t % 2:
            yield from pair_slots(3, t // 2, at + HEADS_LAG[-1])


def tail_events():
    slots = [*last_unit_slots(), *((W_AT + n, ("w", n)) for n in range(4))]
    for s in (0, 1):
        slots += output_slots(s)
    for r, ranges in enumerate(RANGES):
        for s in range(len(ranges)):
            slots += ffn_slots(r, s)
    slots += heads_slots()
    events = [event for _, event in sorted(slots, key=lambda slot: slot[0])]
    for made, used in (("prod", "sum"), ("h", "gelu"), ("h", "g_rest"), ("h", "g2"), ("h", "g3")):
        assert [e[1:] for e in events if e[0] == made] == [e[1:] for e in events if e[0] == used]
    place = {e: n for n, e in enumerate(events)}
    for t in range(TT):
        assert all(place["sum", t, quad] < place["soft", t] for quad in range(QUADS))
    for k in (1, 2, 3):
        for p in range(PAIRS):
            before = [("res_pair", 0, p)] if k == 2 else [("res", k - 1, 2 * p), ("res", k - 1, 2 * p + 1)]
            assert all(place[e] < place["var", k, p] for e in before)
    return events


TAIL_FILLS = ("w", "ao_t", "o", "ao_y", "lnt", "h", "y", "qk", "vs", "bo_y")


def numbered():
    of, count = {}, {}
    events = [(kind, 0, p) for kind in ("var", "norm", "lnt") for p in range(PAIRS)]
    for e in [*events, *tail_events()]:
        of[e] = count.get(e[0], 0)
        count[e[0]] = of[e] + 1
    return of


def ring_place(s, last):
    return s + (s >= SHIFT_AT and not last)


def ring_fills(place, i):
    return (place - i) // len(SCORE_BANKS) + 1


class Banks:

    def __init__(self):
        self.count = [0] * 8
        self.of = {}

    def claim(self, key, bank):
        self.of[key] = (bank, self.count[bank])
        self.count[bank] += 1


def plan_banks():
    banks = Banks()
    for n, key in enumerate([*setup_order(), *beside_max_pass()]):
        banks.claim(key, SETUP_BANKS[n % len(SETUP_BANKS)])
    base = list(banks.count)
    for b in PAIR_BANKS:
        banks.count[b] += NU * FILLS // 2
    for i, b in enumerate(SCORE_BANKS):
        banks.count[b] += (NU - 1) * RING_USES + ring_fills(STEPS - 1, i)
    banks.count[PV_BANK] += NU
    ring, n = BESIDE_LAST_UNIT, 0
    for e in tail_events():
        if e == ("pv", TT - 1):
            ring, n = TAIL_BANKS, 0
        if e[0] == "y":
            banks.claim(e, Y_BANKS[e[2] % 2])
        elif e[0] in TAIL_FILLS:
            banks.claim(e, ring[n % len(ring)])
            n += 1
    return banks.of, base


def build(nc, a):
    uses, base = plan_banks()
    number = numbered()
    events = list(tail_events())
    norms = [e for e in number if e[0] == "norm"]
    kparts_dram = nc.dram_tensor("k_parts", [NPART, DC, P, T], BF16, kind="Internal").ap()
    qparts_dram = nc.dram_tensor("q_parts", [NPART, 2, DC, P, HALF], BF16, kind="Internal").ap()

    with ExitStack() as ctx:
        def sb(name, shape, dt=F32):
            return ctx.enter_context(nc.sbuf_tensor(name, shape, dt))

        def sem(name):
            return ctx.enter_context(nc.semaphore(name))

        x_res = sb("x_res", [P, TT, D])
        xn = sb("xn", [P, 2, 2, D])
        xT = sb("xT", [P, DC, T])
        w_nat = sb("w_nat", [P, 4, DC, D])
        wT = sb("wT", [P, 4, DC, D])
        a_all = sb("a_all", [P, DC, 4, 32])
        b_all = sb("b_all", [P, D])
        aT = sb("aT", [P, D])
        cut = sb("cut", [P, 2, HALF])
        parts = sb("parts", [P, 12 * 1024], BF16)
        k_parts = parts[:, 0:6144].rearrange("p (c a t) -> p c a t", c=DC, a=NPART)
        q_parts = parts[:, 6144:12288].rearrange("p (c h a t) -> p c h a t", c=DC, h=2, a=NPART)
        o_un = parts[:, 0:8192].bitcast(F32).rearrange("p (g t) -> p g t", g=NG)
        pack = sb("pack", [P, 32 * 1024], BF16)
        k_rows = pack[:, 0:16384].rearrange("p (h t) -> p h t", h=H)
        q_rows = pack[:, 16384:32768].rearrange("p (s h t) -> p s h t", s=2, h=H)
        k_group = pack[:, 0:16384].rearrange("p (g j t) -> p g j t", g=NG, j=G)
        q_group = pack[:, 16384:32768].rearrange("p (s g j t) -> p s g j t", s=2, g=NG, j=G)
        g_parts = pack[:, 0:24576].rearrange("p (a f t) -> p a f t", a=NPART, f=FC)
        g_full = pack[:, 24576:28672].bitcast(F32).rearrange("p (r t) -> p r t", r=4)
        qk = wT[:, 0:3, :, :].rearrange("p m c d -> p (m c d)").rearrange("p (r h n) -> p r h n", r=3, h=H)
        v_sb = sb("v_sb", [P, TT, H, HD])
        x12 = v_sb[:, :, :, :].rearrange("p t h d -> p (t h d)").bitcast(F16).rearrange("p (n c t) -> p n c t", n=2, c=DC)
        v_slot = sb("v_slot", [P, 2, TT, G, 32])
        pbuf = sb("pbuf", [P, 2, G, HALF])
        pflat = pbuf[:, :, :, :].rearrange("p a g t -> p (a g t)")
        prod = pflat[:, 0:3072].rearrange("p (r n) -> p r n", r=3)
        late = parts[:, 8192:12288].bitcast(F32)
        o_norm = late[:, 0:512].rearrange("p (r n) -> p r n", r=2)
        oT = late[:, 512:1024].rearrange("p (r c t) -> p r c t", r=2, c=DC)
        probs = late[:, 1024:1536].rearrange("p (r i j) -> p r i j", r=2, i=H)
        s_raw = sb("s_raw", [P, 2, H, H])
        w_out = sb("w_out", [P, DC, D])
        wqkv = w_nat[:, 0:3, :, :].rearrange("p m c d -> p (m c d)").rearrange("p (c n) -> p c n", c=DC)
        w1_nat = sb("w1_nat", [P, FC, D])
        w2_nat = sb("w2_nat", [P, DC, FF])
        w1T = w1_nat[:, 0:4, :].rearrange("p f d -> p (f d)").bitcast(F16).rearrange("p (c f) -> p c f", c=DC)
        w2T = w2_nat[:, 0:1, :].rearrange("p c f -> p (c f)").bitcast(BF16).rearrange("p (f d) -> p f d", f=FC)
        tern1 = sb("tern1", [P, FC, D], BF16)
        tern2 = sb("tern2", [P, DC, FF], BF16)
        below = sb("below", [P, 512], BF16)
        above = sb("above", [P, 512], BF16)
        ident = sb("ident", [P, P])
        identb = sb("identb", [P, P], BF16)
        ones = sb("ones", [P, P])
        onesb = sb("onesb", [P, HALF], BF16)
        causal = sb("causal", [P, H, H])
        kq_bias = sb("kq_bias", [P, 2, DC])
        b1_col = sb("b1_col", [P, FC])
        stats = sb("stats", [P, TT, 6])
        mv = sb("mv", [P, TT, 2])
        rstd = sb("rstd", [P, TT])
        minus_half = sb("minus_half", [P, 2])
        abs_sum = sb("abs_sum", [P, 2])
        thr = sb("thr", [P, 2, 2])
        mx = sb("mx", [P, 2, G * TT // 2])
        mrest = sb("mrest", [P, G * TT // 2])
        m_parts = sb("m_parts", [P, P], BF16)
        m_rows = sb("m_rows", [P, P], BF16)
        rsum = sb("rsum", [P, 2, H])
        hmax = sb("hmax", [P, H])
        hsum = sb("hsum", [P, H])
        w_sum = sb("w_sum", [P, H])
        w_vsum = sb("w_vsum", [P, DC, HD])
        b_vsum = sb("b_vsum", [1, HD])
        bias_flat = pflat[0:1, 0:BIAS_COLS]
        bias_cut = pflat[0:1, BIAS_COLS:BIAS_COLS + NPART * BIAS_COLS // 2].bitcast(BF16) \
            .rearrange("p (a n) -> p a n", a=NPART)
        bias_rows = sb("bias_rows", [NPART, BIAS_COLS], BF16)
        bv_heads = pflat[0:1, 3840:4096].rearrange("p (h n) -> p h n", h=H)
        v_sum = sb("v_sum", [P, 3, HD])

        ps = ctx.enter_context(nc.psum_tensor("ps", [P, 8, 512], F32))

        filled = [sem(f"filled{b}") for b in range(8)]
        drained = [sem(f"drained{b}") for b in range(8)]
        x_in = [sem(f"x_in{p}") for p in range(PAIRS)]
        w_in = [sem(f"w_in{m}") for m in range(4)]
        ab_padded = sem("ab_padded")
        a_in = sem("a_in")
        b_in = sem("b_in")
        bias_scaled = sem("bias_scaled")
        wout_in = sem("wout_in")
        pv_chunk = sem("pv_chunk")
        kq_bias_in = sem("kq_bias_in")
        bias_in = sem("bias_in")
        cols_in = sem("cols_in")
        w1_in = sem("w1_in")
        w2_in = sem("w2_in")
        wqkv_in = sem("wqkv_in")
        ones_rows_in = sem("ones_rows_in")
        consts = sem("consts")
        pads = sem("pads")
        stats_ready = sem("stats_ready")
        rstd_ready = sem("rstd_ready")
        xn_ready = sem("xn_ready")
        rest_ready = sem("rest_ready")
        part_ready = sem("part_ready")
        parts_out = [sem(f"parts_out{i}") for i in range(6)]
        k_packed = [sem(f"k_packed{i}") for i in range(3)]
        q_packed = [sem(f"q_packed{i}") for i in range(5)]
        dve_step = sem("dve_step")
        pool_step = sem("pool_step")
        max_step = sem("max_step")
        shift_split = sem("shift_split")
        shift_landed = sem("shift_landed")
        v_slot_ready = sem("v_slot_ready")
        abs_ready = sem("abs_ready")
        tern_ready = sem("tern_ready")
        x1_ready = sem("x1_ready")
        g_rest = sem("g_rest")
        g2_ready = sem("g2_ready")
        g3_ready = sem("g3_ready")
        products = sem("products")
        reduced = sem("reduced")
        shifted = sem("shifted")
        exped = sem("exped")
        divided = sem("divided")
        bias_split = sem("bias_split")
        bias_rows_in = sem("bias_rows_in")
        vsum_ready = sem("vsum_ready")
        stored = sem("stored")

        def tokens(r, s):
            first, n = RANGES[r][s]
            return slice(P * first, P * (first + n))

        def bank(key):
            return ps[:, uses[key][0], :]

        def to_fill(pe, key):
            b, n = uses[key]
            if n:
                pe.wait_ge(drained[b], n)
            return ps[:, b, :]

        def is_filled(eng, key):
            b, n = uses[key]
            eng.wait_ge(filled[b], n + 1)
            return ps[:, b, :]

        def is_drained(eng, key):
            b, n = uses[key]
            eng.wait_ge(drained[b], n + 1)

        def fill_sem(key):
            return filled[uses[key][0]]

        def drain_sem(key):
            return drained[uses[key][0]]

        def factors(t, quad, out):
            nj, i = 4 * quad + 4, slice(4 * quad, 4 * quad + 4)
            shape = [P, 4, nj, HD]
            in0 = qk[:, t % 3, i, 0:HD].unsqueeze(2).broadcast_to(shape)
            in1 = qk[:, t % 3, 0:nj, HD:2 * HD].unsqueeze(1).broadcast_to(shape)
            return in0, in1, out[:, 0:4 * nj * HD].rearrange("p (i j n) -> p i j n", i=4, j=nj)

        block = ctx.enter_context(nc.Block())

        @block.sync
        def _(sp):
            xv = a["L0_attn_a_x"].rearrange("o (t p) d -> (o p) t d", p=P)
            for p in range(PAIRS):
                sp.dma_start(x_res[:, 2 * p:2 * p + 2, :], xv[:, 2 * p:2 * p + 2, :]).then_inc(x_in[p], 16)
            for m, name in ((Q_, "Wq"), (V_, "Wv"), (O_, "Wo")):
                sp.dma_start(w_nat[:, m, :, :],
                             a[f"L0_attn_a_{name}"].rearrange("(c p) d -> p c d", p=P)).then_inc(w_in[m], 16)
            for n, name in enumerate(("bk", "bq")):
                t = a[f"L0_attn_a_{name}"].tensor
                for c in range(DC):
                    sp.dma_start(kq_bias[:, n, c:c + 1], bass.AP(t, P * c, [[1, HD], [HD, HC], [1, 1]]),
                                 allow_slow_non_contiguous=True).then_inc(kq_bias_in, 16)
            bqkv = a["L0_attn_b_bqkv"]
            sp.dma_start(bias_flat[:, 0:H * 2 * HD].rearrange("o (h n) -> o h n", h=H), bqkv[:, 0:2 * HD].unsqueeze(0)) \
                .then_inc(bias_in, 16)
            sp.dma_start(bv_heads, bqkv[:, 2 * HD:3 * HD].unsqueeze(0)).then_inc(bias_in, 16)
            for which, name in (("bo", "L0_attn_a_bo"), ("b2", "L0_ffn_b2"), ("bout", "L0_attn_b_bout"), ("bv", "L0_attn_a_bv")):
                at = BIAS_AT[which]
                sp.dma_start(bias_flat[:, at:at + D], a[name].rearrange("(a n) -> a n", a=1)).then_inc(bias_in, 16)
            sp.dma_start(w1_nat[:, :, :], a["L0_ffn_w1"].rearrange("(f p) d -> p f d", p=P)).then_inc(w1_in, 16)
            sp.dma_start(w2_nat[:, :, :], a["L0_ffn_w2"].rearrange("(c p) f -> p c f", p=P)).then_inc(w2_in, 16)
            sp.dma_start(b1_col[:, :], a["L0_ffn_b1"].rearrange("(f p) -> p f", p=P),
                         allow_slow_non_contiguous=True).then_inc(cols_in, 16)
            sp.dma_start(w_out[:, :, :], a["L0_attn_b_Wout"].rearrange("h d m -> (h d) m")
                         .rearrange("(c p) m -> p c m", p=P)).then_inc(wout_in, 16)
            sp.wait_ge(bias_split, 1)
            sp.dma_start(bias_rows[:, :], bias_cut.rearrange("o a n -> o (a n)")).then_inc(bias_rows_in, 16)
            sp.wait_ge(consts, 4)
            for j in range(NPART):
                sp.dma_start(k_rows[ROWS + j:ROWS + j + 1, :, :].rearrange("o h t -> o (h t)"),
                             onesb[0:H * T // HALF, :]).then_inc(ones_rows_in, 16)

            def store_k(n, c):
                sp.wait_ge(part_ready, 2 if c == 0 else 6)
                sp.dma_start(kparts_dram[:, c, :, :].rearrange("a f t -> f a t"), k_parts[:, c, :, :]) \
                    .then_inc(parts_out[n], 16)

            def store_q(n, c, s):
                sp.wait_ge(part_ready, ITEMS.index((Q_, c, s)) + 1)
                sp.dma_start(qparts_dram[:, s, c, :, :].rearrange("a f t -> f a t"), q_parts[:, c, s, :, :]) \
                    .then_inc(parts_out[n], 16)

            def pack_k(n, c, h0, nh, done):
                sp.wait_ge(parts_out[n], 16)
                at = kparts_dram[0:1, c:c + 1, :, :].offset + h0 * T
                for row, first, count in ((0, 0, 3), (3, 0, 3), (6, 0, 1)):
                    src = bass.AP(kparts_dram.tensor, at + first * DC * P * T,
                                  [[DC * P * T, count], [HC * T, HD], [1, nh * T]])
                    sp.dma_start(k_rows[row * HD:(row + count) * HD, HC * c + h0:HC * c + h0 + nh, :]
                                 .rearrange("p h t -> p (h t)"), src).then_inc(done, 16)

            def pack_q(n, c, s, h0, nh, done):
                sp.wait_ge(parts_out[n], 16)
                at = qparts_dram[0:1, s:s + 1, c:c + 1, :, :].offset + h0 * HALF
                for row, part, count in ((0, 0, 3), (3, 1, 3), (6, 2, 1)):
                    src = bass.AP(qparts_dram.tensor, at + part * 2 * DC * P * HALF,
                                  [[0, count], [HC * HALF, HD], [1, nh * HALF]])
                    sp.dma_start(q_rows[row * HD:(row + count) * HD, s, HC * c + h0:HC * c + h0 + nh, :]
                                 .rearrange("p h t -> p (h t)"), src).then_inc(done, 16)

            store_k(0, 0)
            store_q(1, 0, 0)
            pack_k(0, 0, 0, G, k_packed[0])
            pack_q(1, 0, 0, 0, G, q_packed[0])
            store_q(2, 0, 1)
            pack_q(2, 0, 1, 0, HC, q_packed[1])
            pack_k(0, 0, G, G, k_packed[1])
            pack_q(1, 0, 0, G, G, q_packed[2])
            store_k(3, 1)
            store_q(4, 1, 0)
            store_q(5, 1, 1)

            def land_shift(g, qh, u):
                if isinstance(u, int) and u == 0:
                    is_drained(sp, ("shift",))
                else:
                    i = SHIFT_AT % len(SCORE_BANKS)
                    b = SCORE_BANKS[i]
                    sp.wait_ge(drained[b], u * RING_USES + (base[b] + ring_fills(SHIFT_AT, i) - RING_USES))
                n = G * TT // 2
                for j in range(NPART):
                    sp.dma_start(q_rows[ROWS + j:ROWS + j + 1, qh, bass.ds(g * G, G), :]
                                 .rearrange("o h t -> o (h t)"), m_rows[n * j:n * j + n, :]) \
                        .then_inc(shift_landed, 16)

            land_shift(0, 0, 0)
            pack_k(3, 1, 0, HC, k_packed[2])
            pack_q(4, 1, 0, 0, HC, q_packed[3])
            pack_q(5, 1, 1, 0, HC, q_packed[4])
            with sp.Fori(0, NG - 1) as g:
                land_shift(g, 1, g * 2 + 1)
                land_shift(g + 1, 0, g * 2 + 2)
            land_shift(NG - 1, 1, NU - 1)

            ov = a["out"].rearrange("o (t p) d -> (o p) t d", p=P)
            for p in range(PAIRS):
                is_drained(sp, ("y", 1, p))
                sp.dma_start(ov[:, 2 * p:2 * p + 2, :], x_res[:, 2 * p:2 * p + 2, :]).then_inc(stored, 16)
            sp.wait_ge(stored, 16 * PAIRS)

        @block.gpsimd
        def _(pool):
            steps = [0]

            def link(ins):
                steps[0] += 1
                ins.then_inc(pool_step, 1)
                pool.wait_ge(pool_step, steps[0])

            def eye(t):
                link(pool.memset(t[:, :], 0.0))
                pool.affine_select(out=t[:, :], in_=t[:, :], compare_op=ALU.not_equal, fill=1.0, base=0,
                                   pattern=[[-1, P]], channel_multiplier=1).then_inc(consts, 1)

            pool.memset(minus_half[:, :], -0.5).then_inc(consts, 1)
            eye(ident)
            pool.memset(ones[:, :], 1.0).then_inc(consts, 1)
            pool.memset(onesb[:, :], 1.0).then_inc(consts, 1)
            eye(identb)

            pool.wait_ge(consts, 5)

            def inverse_deviations(k, p):
                pool.wait_ge(stats_ready, number["var", k, p] + 1)
                pool.tensor_tensor(rstd[:, 2 * p:2 * p + 2], rstd[:, 2 * p:2 * p + 2], minus_half[:, :], ALU.pow) \
                    .then_inc(rstd_ready, 1)

            for p in range(PAIRS):
                inverse_deviations(0, p)

            def third_part(i):
                m, c, s = ITEMS[i]
                dst = k_parts[:, c, 2, HALF * s:HALF * s + HALF] if m == K_ else q_parts[:, c, s, 2, :]
                mid = k_parts[:, c, 1, HALF * s:HALF * s + HALF] if m == K_ else q_parts[:, c, s, 1, :]
                pool.wait_ge(rest_ready, i + 1)
                pool.tensor_tensor(dst, cut[:, i % 2, :], mid, ALU.subtract).then_inc(part_ready, 1)

            for i in range(len(ITEMS)):
                third_part(i)
            pool.memset(v_slot[:, :, :, :, HD:32], 1.0).then_inc(pads, 1)
            pool.memset(s_raw[:, :, :, :], 0.0).then_inc(pads, 1)
            link(pool.memset(causal[:, :, :], 0.0))
            pool.affine_select(out=causal[:, :, :], in_=causal[:, :, :], compare_op=ALU.is_ge, fill=NEG, base=0,
                               pattern=[[1, H], [-1, H]], channel_multiplier=0).then_inc(consts, 1)


            is_drained(pool, ("wsum",))
            for n, (w, tern) in enumerate(((w1_nat, tern1), (w2_nat, tern2))):
                wf = w[:, :, :].rearrange("p c d -> p (c d)")
                tf = tern[:, :, :].rearrange("p c d -> p (c d)")
                for c in range(4):
                    v = slice(512 * c, 512 * c + 512)
                    link(pool.tensor_scalar(below[:, :], wf[:, v], thr[:, n, 1:2], None, ALU.is_lt))
                    link(pool.tensor_scalar(above[:, :], wf[:, v], thr[:, n, 0:1], None, ALU.is_gt))
                    pool.tensor_tensor(tf[:, v], above[:, :], below[:, :], ALU.subtract).then_inc(tern_ready, 1)
                    pool.wait_ge(tern_ready, 4 * n + c + 1)

            def third_gelu_part(r, s, f):
                n = number["h", r, s, f]
                pool.wait_ge(g2_ready, n + 1)
                v = tokens(r, s)
                pool.tensor_tensor(g_parts[:, 2, f, v], g_full[:, n % 4, 0:v.stop - v.start], g_parts[:, 1, f, v], ALU.subtract) \
                    .then_inc(g3_ready, 1)

            made = [0]

            def product(t, quad):
                if quad == QUADS - 1:
                    is_drained(pool, ("qk", t))
                if made[0] >= 3:
                    pool.wait_ge(reduced, made[0] - 2)
                in0, in1, out = factors(t, quad, prod[:, made[0] % 3, :])
                pool.tensor_tensor(out, in0, in1, ALU.mult).then_inc(products, 1)
                made[0] += 1

            for e in events:
                if e[0] == "var":
                    inverse_deviations(*e[1:])
                if e[0] == "g3":
                    third_gelu_part(*e[1:])
                if e[0] == "prod":
                    product(e[1], e[2])

        @block.scalar
        def _(act):
            act.wait_ge(ab_padded, 1)
            for m, n in ((K_, "k"), (Q_, "q"), (V_, "v"), (O_, "o")):
                act.dma_start(a_all[:, :, m, 0:RANK], a[f"L0_attn_a_A{n}"].rearrange("(c p) r -> p c r", p=P)) \
                    .then_inc(a_in, 16)
            act.dma_start(w_nat[:, K_, :, :], a["L0_attn_a_Wk"].rearrange("(c p) d -> p c d", p=P)).then_inc(w_in[K_], 16)
            for m, n in ((K_, "k"), (Q_, "q"), (V_, "v"), (O_, "o")):
                act.dma_start(b_all[32 * m:32 * m + RANK, :], a[f"L0_attn_a_B{n}"]).then_inc(b_in, 16)

            is_filled(act, ("at",))
            act.mul(aT[:, :], bank(("at",))[:, 0:D], LORA_SCALE).then_inc(drain_sem(("at",)), 1)

            def evacuate_lnt(k, p):
                src = is_filled(act, ("lnt", k, p)).rearrange("p (c t) -> p c t", c=DC)
                act.copy(xT[:, :, 256 * p:256 * p + 256], src).then_inc(drain_sem(("lnt", k, p)), 1)

            def evacuate_weight(m):
                key = ("wt", m)
                src = is_filled(act, key)
                if m in (K_, Q_):
                    for c in range(DC):
                        ins = act.copy(wT[:, m, c, :].rearrange("p (f d h) -> p f d h", f=DC, d=HD),
                                       src[:, D * c:D * c + D].rearrange("p (f h d) -> p f d h", f=DC, h=HC))
                else:
                    ins = act.copy(wT[:, m, :, :], src.rearrange("p (c n) -> p c n", c=DC))
                ins.then_inc(drain_sem(key), 1)

            def project_out(i):
                m, c, s = ITEMS[i]
                key = ("proj", i)
                src = is_filled(act, key)
                if i >= 2:
                    act.wait_ge(part_ready, i - 1)
                first = k_parts[:, c, 0, HALF * s:HALF * s + HALF] if m == K_ else q_parts[:, c, s, 0, :]
                scale = 1.0 if m == K_ else SCALE
                bias = kq_bias[:, 0 if m == K_ else 1, c:c + 1]
                act.activation(cut[:, i % 2, :], src, ACT.Identity, bias=bias, scale=scale)
                act.activation(first, src, ACT.Identity, bias=bias, scale=scale).then_inc(drain_sem(key), 1)

            for key in setup_order():
                if key[0] == "lnt":
                    evacuate_lnt(*key[1:])
                if key[0] == "wt":
                    evacuate_weight(key[1])
                if key == ("proj", 0):
                    act.wait_ge(kq_bias_in, 64)
                    act.mul(kq_bias[:, 1, :], kq_bias[:, 1, :], SCALE).then_inc(bias_scaled, 1)
                    act.wait_ge(bias_scaled, 1)
                if key[0] == "proj":
                    project_out(key[1])
            act.dma_start(wqkv[:, :, :], a["L0_attn_b_Wqkv"].rearrange("(c p) h n -> p c (h n)", p=P)).then_inc(wqkv_in, 16)
            for t in range(TT):
                key = ("v", t)
                src = is_filled(act, key)
                act.copy(v_sb[:, t, :, :], src[:, 0:D].rearrange("p (h d) -> p h d", h=H)).then_inc(drain_sem(key), 1)
                if t == 1:
                    act.wait_ge(w1_in, 16)
                    act.wait_ge(w2_in, 16)
                    act.wait_ge(bias_rows_in, 16)
                    act.activation(pflat[:, 0:2048], w1_nat[:, :, :].rearrange("p f d -> p (f d)"), ACT.Abs,
                                   accum_out=abs_sum[:, 0:1]).then_inc(abs_ready, 1)
                    act.activation(pflat[:, 2048:4096], w2_nat[:, :, :].rearrange("p c f -> p (c f)"), ACT.Abs,
                                   accum_out=abs_sum[:, 1:2]).then_inc(abs_ready, 1)
            act.wait_ge(cols_in, 16)

            def copy_shift(u):
                if isinstance(u, int) and u == 0:
                    key = ("shift",)
                    src = is_filled(act, key)[:, 0:P // 2].bitcast(BF16)
                    act.copy(m_rows[:, :], src).then_inc(drain_sem(key), 1)
                    return
                i = SHIFT_AT % len(SCORE_BANKS)
                b = SCORE_BANKS[i]
                act.wait_ge(filled[b], u * RING_USES + (base[b] + ring_fills(SHIFT_AT, i) - RING_USES))
                act.copy(m_rows[:, :], ps[:, b, 0:P // 2].bitcast(BF16)).then_inc(drained[b], 1)

            def evacuate_pv(g, qh, u):
                act.wait_ge(filled[PV_BANK], base[PV_BANK] + u + 1)
                act.copy(o_un[:, bass.ds(g, 1), HALF * qh:HALF * qh + HALF].rearrange("p g t -> p (g t)"),
                         ps[:, PV_BANK, :]).then_inc(drained[PV_BANK], 1)

            def exp_tile(u, s):
                c, j = divmod(s, G)
                place = ring_place(s, isinstance(u, int) and u == NU - 1)
                i = place % len(SCORE_BANKS)
                b = SCORE_BANKS[i]
                act.wait_ge(filled[b], base[b] + u * RING_USES + ring_fills(place, i))
                if j == 0 and not (isinstance(u, int) and u == 0 and c < 2):
                    if c == 1:
                        act.wait_ge(filled[PV_BANK], base[PV_BANK] + u)
                    else:
                        act.wait_ge(pv_chunk, u * (TT - 1) + (c - 1 if c else 0))
                act.activation(pbuf[:, c % 2, j, :], ps[:, b, :], ACT.Exp).then_inc(drained[b], 1)

            def exp_unit(g, qh, u, more=True):
                for s in range(G, STEPS):
                    if s == SHIFT_AT:
                        copy_shift(u + 1)
                    exp_tile(u, s)
                for s in range(G):
                    exp_tile(u + 1, s)
                evacuate_pv(g, qh, u)
                if more:
                    act.copy(v_slot[:, qh, :, :, 0:HD], v_sb[:, :, bass.ds((g + 1) * G, G), :]).then_inc(v_slot_ready, 1)

            copy_shift(0)
            for t in range(TT):
                is_drained(act, ("v", t))
            act.wait_ge(pads, 1)
            for qh in (0, 1):
                act.copy(v_slot[:, qh, :, :, 0:HD], v_sb[:, :, 0:G, :]).then_inc(v_slot_ready, 1)
            for s in range(G):
                exp_tile(0, s)
            for n in (3, 4, 5):
                act.wait_ge(parts_out[n], 16)
            with act.Fori(0, NG - 1) as g:
                exp_unit(g, 0, g * 2)
                exp_unit(g, 1, g * 2 + 1)
            exp_unit(NG - 1, 0, NU - 2, more=False)

            def o_out(key):
                act.copy(oT[:, number[key] % 2, :, :], is_filled(act, key)[:, 0:D].rearrange("p (c t) -> p c t", c=DC)) \
                    .then_inc(drain_sem(key), 1)

            def first_x_part(k, p):
                src = is_filled(act, ("lnt", k, p)).rearrange("p (c t) -> p c t", c=DC)
                act.mul(x12[:, 0, :, 256 * p:256 * p + 256], src, X_SCALE).then_inc(x1_ready, 1)

            def gelu(key):
                _, r, s, f = key
                src = is_filled(act, key)
                n = number[key]
                if n >= 4:
                    act.wait_ge(g3_ready, n - 3)
                v = tokens(r, s)
                src = src[:, 0:v.stop - v.start]
                act.activation(g_full[:, n % 4, 0:v.stop - v.start], src, ACT.Gelu, bias=b1_col[:, f:f + 1])
                act.activation(g_parts[:, 0, f, v], src, ACT.Gelu, bias=b1_col[:, f:f + 1]) \
                    .then_inc(drain_sem(key), 1)

            def gelu_second(r, s, f):
                n = number["h", r, s, f]
                act.wait_ge(g_rest, n + 1)
                v = tokens(r, s)
                act.copy(g_parts[:, 1, f, v], g_full[:, n % 4, 0:v.stop - v.start]).then_inc(g2_ready, 1)

            def qk_out(t):
                if t >= 3:
                    act.wait_ge(divided, t - 2)
                act.copy(qk[:, t % 3, :, :].rearrange("p h n -> p (h n)"), is_filled(act, ("qk", t))) \
                    .then_inc(drain_sem(("qk", t)), 1)

            def vs_out(t):
                act.copy(v_sum[:, t % 3, :], is_filled(act, ("vs", t))[:, 0:HD]).then_inc(drain_sem(("vs", t)), 1)

            def exp_heads(t):
                act.wait_ge(shifted, t + 1)
                act.activation(probs[:, t % 2, :, :], probs[:, t % 2, :, :], ACT.Exp, scale=SCALE).then_inc(exped, 1)

            for e in events:
                if e[0] == "exp":
                    exp_tile(NU - 1, e[1])
                if e[0] == "pv_out":
                    evacuate_pv(NG - 1, 1, NU - 1)
                if e[0] == "o_out":
                    o_out(("o", *e[1:]))
                if e[0] == "lnt_out":
                    (evacuate_lnt if e[1] == 2 else first_x_part)(*e[1:])
                if e[0] == "gelu":
                    gelu(("h", *e[1:]))
                if e[0] == "g2":
                    gelu_second(*e[1:])
                if e[0] == "qk_out":
                    qk_out(e[1])
                if e[0] == "vs_out":
                    vs_out(e[1])
                if e[0] == "exp_heads":
                    exp_heads(e[1])

        @block.vector
        def _(dve):
            steps = [0]

            def link(ins):
                steps[0] += 1
                ins.then_inc(dve_step, 1)
                dve.wait_ge(dve_step, steps[0])

            dve.memset(m_parts[:, :], 0.0)
            link(dve.memset(a_all[:, :, :, :].rearrange("p c m r -> p (c m r)"), 0.0))
            dve.memset(b_all[:, :], 0.0).then_inc(ab_padded, 1)

            def variances(k, p):
                if k == 0:
                    dve.wait_ge(x_in[p], 16)
                for t in (2 * p, 2 * p + 1):
                    dve.bn_stats(stats[:, t, :], x_res[:, t, :]).then_inc(dve_step, 1)
                    steps[0] += 1
                dve.wait_ge(dve_step, steps[0])
                for t in (2 * p, 2 * p + 1):
                    dve.bn_aggr(mv[:, t, :], stats[:, t, :]).then_inc(dve_step, 1)
                    steps[0] += 1
                dve.wait_ge(dve_step, steps[0])
                dve.tensor_scalar(rstd[:, 2 * p:2 * p + 2], mv[:, 2 * p:2 * p + 2, 1], EPS, None, ALU.add) \
                    .then_inc(stats_ready, 1)

            def normalise(k, p):
                n = number["norm", k, p]
                dve.wait_ge(rstd_ready, number["var", k, p] + 1)
                if n >= 2:
                    is_filled(dve, ("lnt", *norms[n - 2][1:]))
                for i in (0, 1):
                    t = 2 * p + i
                    ins = dve.tensor_scalar(xn[:, n % 2, i, :], x_res[:, t, :], mv[:, t, 0:1], rstd[:, t:t + 1],
                                            ALU.subtract, ALU.mult)
                ins.then_inc(xn_ready, 1)

            variances(0, 0)
            for p in range(PAIRS):
                if p + 1 < PAIRS:
                    variances(0, p + 1)
                normalise(0, p)

            dve.wait_ge(bias_in, 16 * 6)
            dve.tensor_reduce(b_vsum[:, :], bv_heads.rearrange("o h n -> o n h"), AX_X, ALU.add)
            link(dve.tensor_copy(bias_cut[:, 0, :], bias_flat))
            link(dve.tensor_tensor(bias_flat, bias_flat, bias_cut[:, 0, :], ALU.subtract))
            link(dve.tensor_copy(bias_cut[:, 1, :], bias_flat))
            dve.tensor_tensor(bias_cut[:, 2, :], bias_flat, bias_cut[:, 1, :], ALU.subtract).then_inc(bias_split, 1)

            def middle_part(i):
                m, c, s = ITEMS[i]
                v = slice(HALF * s, HALF * s + HALF)
                one = k_parts[:, c, 0, v] if m == K_ else q_parts[:, c, s, 0, :]
                two = k_parts[:, c, 1, v] if m == K_ else q_parts[:, c, s, 1, :]
                is_drained(dve, ("proj", i))
                link(dve.tensor_tensor(cut[:, i % 2, :], cut[:, i % 2, :], one, ALU.subtract))
                dve.tensor_copy(two, cut[:, i % 2, :]).then_inc(rest_ready, 1)

            for i in range(len(ITEMS)):
                middle_part(i)

            n_max = G * TT // 2

            def m_part(n):
                return m_parts[:, n_max * n:n_max * n + n_max]


            def take_max(u, k, par):
                b = PAIR_BANKS[k % 2]
                dve.wait_ge(filled[b], base[b] + u * (FILLS // 2) + (k // 2 + 1))
                dve.tensor_reduce(mx[:, par, k:k + 1], ps[:, b:b + 2, :].rearrange("p b k -> p (b k)"), AX_X, ALU.max) \
                    .then_inc(drained[b], 1)

            def cut_max(u, par):
                for b in PAIR_BANKS:
                    dve.wait_ge(drained[b], base[b] + u * (FILLS // 2) + FILLS // 2)
                dve.tensor_scalar(m_part(0), mx[:, par, :], -1.0, None, ALU.mult).then_inc(max_step, 1)
                dve.wait_ge(max_step, u * 3 + 1)
                dve.scalar_tensor_tensor(out=mrest[:, :], in0=mx[:, par, :], scalar=-1.0, in1=m_part(0),
                                         op0=ALU.mult, op1=ALU.subtract).then_inc(max_step, 1)
                dve.wait_ge(max_step, u * 3 + 2)
                dve.tensor_copy(m_part(1), mrest[:, :]).then_inc(max_step, 1)
                dve.wait_ge(max_step, u * 3 + 3)
                dve.tensor_tensor(m_part(2), mrest[:, :], m_part(1), ALU.subtract).then_inc(shift_split, 1)

            for k in range(FILLS):
                take_max(0, k, 0)
            cut_max(0, 0)
            src = is_filled(dve, ("wsum",))
            dve.tensor_scalar(thr[:, :, 0], src[:, 0:2], 0.5 / (FF * D), 0.5 * WQ_EPS, ALU.mult, ALU.max)
            dve.tensor_scalar(thr[:, :, 1], src[:, 0:2], -0.5 / (FF * D), -0.5 * WQ_EPS, ALU.mult, ALU.min) \
                .then_inc(drain_sem(("wsum",)), 1)
            for k in range(LEAD):
                take_max(1, k, 1)

            def unit_max(u, next_par):
                for k in range(LEAD, FILLS):
                    take_max(u + 1, k, next_par)
                cut_max(u + 1, next_par)

            def lead_max(u, par):
                for k in range(LEAD):
                    take_max(u, k, par)

            with dve.Fori(0, NG - 1) as g:
                unit_max(g * 2, 1)
                lead_max(g * 2 + 2, 0)
                unit_max(g * 2 + 1, 0)
                lead_max(g * 2 + 3, 1)
            unit_max(NU - 2, 1)

            def residual(r, t, key):
                src = is_filled(dve, key)
                dve.tensor_tensor(x_res[:, t, :], src[:, 0:D], x_res[:, t, :], ALU.add).then_inc(drain_sem(key), 1)
                if t % 2 == 1:
                    is_drained(dve, key)

            def ternary_out(n):
                c, key = n // 2, ("w", n)
                src = is_filled(dve, key).bitcast(BF16)
                if n % 2 == 0:
                    dve.tensor_scalar(w1T[:, c, :], src, 1.0 / X_SCALE, None, ALU.mult).then_inc(drain_sem(key), 1)
                else:
                    dve.tensor_copy(w2T[:, 4 * c:4 * c + 4, :].rearrange("p f d -> p (f d)"), src) \
                        .then_inc(drain_sem(key), 1)

            def residual_pair(r, p):
                key = ("y", r, p)
                src = is_filled(dve, key).rearrange("p (t d) -> p t d", t=2)
                pair = x_res[:, 2 * p:2 * p + 2, :]
                dve.tensor_tensor(pair, src, pair, ALU.add).then_inc(drain_sem(key), 1)
                if r == 0:
                    is_drained(dve, key)

            def divide(key):
                t = key[1]
                src = is_filled(dve, key).rearrange("p (h n) -> p h n", h=H)
                link(dve.reciprocal(rsum[:, t % 2, :], src[:, :, HD]))
                n = number["o", "a", t]
                if n >= 2:
                    is_filled(dve, outs[n - 2])
                dve.tensor_tensor(o_norm[:, n % 2, :].rearrange("p (h n) -> p h n", h=H), src[:, :, 0:HD],
                                  rsum[:, t % 2, :].unsqueeze(2).broadcast_to([P, H, HD]), ALU.mult) \
                    .then_inc(drain_sem(key), 1)

            def second_x_part(k, p):
                key = ("lnt", k, p)
                is_filled(dve, key)
                dve.wait_ge(x1_ready, x12_pairs.index(key) + 1)
                v = slice(256 * p, 256 * p + 256)
                dve.scalar_tensor_tensor(out=x12[:, 1, :, v], in0=bank(key).rearrange("p (c t) -> p c t", c=DC),
                                         scalar=X_SCALE, in1=x12[:, 0, :, v], op0=ALU.mult, op1=ALU.subtract) \
                    .then_inc(drain_sem(key), 1)

            def gelu_rest(r, s, f):
                is_drained(dve, ("h", r, s, f))
                v = tokens(r, s)
                g = g_full[:, number["h", r, s, f] % 4, 0:v.stop - v.start]
                dve.tensor_tensor(g, g, g_parts[:, 0, f, v], ALU.subtract).then_inc(g_rest, 1)

            taken = [0]

            def head_scores(t, quad):
                nj, i = 4 * quad + 4, slice(4 * quad, 4 * quad + 4)
                slot = prod[:, taken[0] % 3, :]
                taken[0] += 1
                dve.wait_ge(products, taken[0])
                _, _, terms = factors(t, quad, slot)
                dve.tensor_reduce(s_raw[:, t % 2, i, 0:nj], terms, AX_X, ALU.add).then_inc(reduced, 1)

            def soften(t):
                dve.wait_ge(reduced, taken[0])
                p = probs[:, t % 2, :, :]
                link(dve.tensor_tensor(p, s_raw[:, t % 2, :, :], causal[:, :, :], ALU.add))
                link(dve.tensor_reduce(hmax[:, :], p, AX_X, ALU.max))
                dve.tensor_tensor(p, p, hmax[:, :].unsqueeze(2).broadcast_to([P, H, H]), ALU.subtract).then_inc(shifted, 1)

            def head_outputs(t):
                w = probs[:, t % 2, :, :]
                dve.wait_ge(exped, t + 1)
                link(dve.tensor_reduce(hsum[:, :], w, AX_X, ALU.add))
                link(dve.reciprocal(hsum[:, :], hsum[:, :]))
                link(dve.tensor_tensor(w, w, hsum[:, :].unsqueeze(2).broadcast_to([P, H, H]), ALU.mult))
                link(dve.tensor_reduce(w_sum[:, :], w, AX_X, ALU.add))
                n = number["o", "b", t]
                is_drained(dve, ("vs", t))
                is_filled(dve, outs[n - 2])
                dve.tensor_tensor(o_norm[:, n % 2, :].rearrange("p (h n) -> p h n", h=H),
                                  w_sum[:, :].unsqueeze(2).broadcast_to([P, H, HD]),
                                  v_sum[:, t % 3, :].unsqueeze(1).broadcast_to([P, H, HD]), ALU.mult).then_inc(divided, 1)

            outs = [e for e in events if e[0] == "o"]
            x12_pairs = [e for e in events if e[0] == "lnt" and e[1] != 2]
            dve.wait_ge(wqkv_in, 16)
            wv = wqkv[:, :, :].rearrange("p c (h n) -> p c n h", h=H)[:, :, 2 * HD:3 * HD, :]
            dve.tensor_reduce(w_vsum[:, :, :], wv, AX_X, ALU.add).then_inc(vsum_ready, 1)
            dve.wait_ge(pads, 2)
            dve.wait_ge(consts, 6)
            for e in events:
                if e[0] == "w":
                    ternary_out(e[1])
                if e[0] == "div":
                    divide(("ao_t", e[1]))
                if e[0] == "res":
                    r, t = e[1:]
                    residual(r, t, ("ao_y", t) if r == 0 else ("bo_y", t))
                if e[0] == "res_pair":
                    residual_pair(*e[1:])
                if e[0] == "var":
                    variances(*e[1:])
                if e[0] == "norm":
                    normalise(*e[1:])
                if e[0] == "x_rest":
                    second_x_part(*e[1:])
                if e[0] == "g_rest":
                    gelu_rest(*e[1:])
                if e[0] == "sum":
                    head_scores(e[1], e[2])
                if e[0] == "soft":
                    soften(e[1])
                if e[0] == "wv":
                    head_outputs(e[1])

        @block.tensor
        def _(pe):
            def lora_a_transposed(key):
                pe.wait_ge(consts, 2)
                pe.wait_ge(a_in, 16 * 4)
                out = to_fill(pe, key)
                for c in range(DC):
                    ins = pe.transpose(out[:, P * c:P * c + P], a_all[:, c, :, :].rearrange("p m r -> p (m r)"), ident[:, :])
                ins.then_inc(fill_sem(key), 1)

            def merged_weight(key):
                m = key[1]
                if m == K_:
                    is_drained(pe, ("at",))
                    pe.wait_ge(b_in, 16 * 4)
                pe.wait_ge(w_in[m], 16)
                out = to_fill(pe, key)
                r = slice(32 * m, 32 * m + RANK)
                for c in range(DC):
                    pe.matmul(out[:, D * c:D * c + D], b_all[r, P * c:P * c + P], aT[r, :], start=True, stop=False)
                    for o in range(DC):
                        ins = pe.matmul(out[:, D * c + P * o:D * c + P * o + P], w_nat[:, m, o, P * c:P * c + P],
                                        ident[:, :], start=False, stop=(o == DC - 1))
                ins.then_inc(fill_sem(key), 1)

            def transpose_pair(key):
                _, k, p = key
                n = number["norm", k, p]
                pe.wait_ge(xn_ready, n + 1)
                out = to_fill(pe, key)
                for c in range(DC):
                    for i in (0, 1):
                        ins = pe.transpose(out[:, 256 * c + P * i:256 * c + P * i + P], xn[:, n % 2, i, P * c:P * c + P],
                                           ident[:, :])
                ins.then_inc(fill_sem(key), 1)

            def project(key):
                m, c, s = ITEMS[key[1]]
                if key[1] == 0:
                    for w in (K_, Q_):
                        is_drained(pe, ("wt", w))
                for p in (2 * s, 2 * s + 1):
                    is_drained(pe, ("lnt", 0, p))
                out = to_fill(pe, key)
                for d in range(DC):
                    ins = pe.matmul(out, wT[:, m, d, P * c:P * c + P], xT[:, d, HALF * s:HALF * s + HALF],
                                    start=(d == 0), stop=(d == DC - 1))
                ins.then_inc(fill_sem(key), 1)

            def add_bias(out, which):
                at, n = BIAS_AT[which], 512 if which == "qk" else D
                pe.matmul(out, onesb[0:NPART, 0:P], bias_rows[:, at:at + n], start=True, stop=False)

            def project_v(key):
                t = key[1]
                if t == 0:
                    is_drained(pe, ("wt", V_))
                    pe.wait_ge(bias_rows_in, 16)
                    pe.wait_ge(consts, 4)
                out = to_fill(pe, key)[:, 0:D]
                add_bias(out, "bv")
                for d in range(DC):
                    ins = pe.matmul(out, xT[:, d, P * t:P * t + P], wT[:, V_, d, :], start=False, stop=(d == DC - 1))
                ins.then_inc(fill_sem(key), 1)

            def weight_sums(key):
                pe.wait_ge(abs_ready, 2)
                out = to_fill(pe, key)
                pe.matmul(out[:, 0:2], ones[:, :], abs_sum[:, :], start=True, stop=True).then_inc(fill_sem(key), 1)

            setup = {"at": lora_a_transposed, "wt": merged_weight, "lnt": transpose_pair, "proj": project,
                     "v": project_v, "wsum": weight_sums}
            for key in setup_order():
                setup[key[0]](key)

            def max_tile(g, qh, u, k):
                j, qt = divmod(k, TT // 2)
                b = PAIR_BANKS[k % 2]
                at = bass.ds(g, 1)
                if isinstance(u, int) and u == 0 and k < 2:
                    pass
                else:
                    pe.wait_ge(drained[b], base[b] + u * (FILLS // 2) + k // 2)
                for n in (0, 1):
                    ins = pe.matmul(ps[:, b + n, :], q_group[0:ROWS, qh, at, j, P * qt:P * qt + P].rearrange("p g t -> p (g t)"),
                                    k_group[0:ROWS, at, j, HALF * n:HALF * n + HALF].rearrange("p g t -> p (g t)"),
                                    start=True, stop=True)
                ins.then_inc(filled[b], 1)

            def shift_rows(u):
                pe.wait_ge(shift_split, u + 1)
                if isinstance(u, int) and u == 0:
                    b = uses["shift",][0]
                    to_fill(pe, ("shift",))
                else:
                    i = SHIFT_AT % len(SCORE_BANKS)
                    b = SCORE_BANKS[i]
                    pe.wait_ge(drained[b], u * RING_USES + (base[b] + ring_fills(SHIFT_AT, i) - RING_USES - 1))
                pe.transpose(ps[:, b, 0:P // 2].bitcast(BF16), m_parts[:, :], identb[:, :]).then_inc(filled[b], 1)

            def score_tile(g, qh, u, s):
                c, j = divmod(s, G)
                place = ring_place(s, isinstance(u, int) and u == NU - 1)
                i = place % len(SCORE_BANKS)
                b = SCORE_BANKS[i]
                pe.wait_ge(drained[b], base[b] + u * RING_USES + (ring_fills(place, i) - 1))
                at = bass.ds(g, 1)
                pe.matmul(ps[:, b, :], k_group[0:SROWS, at, j, P * c:P * c + P].rearrange("p g t -> p (g t)"),
                          q_group[0:SROWS, qh, at, j, :].rearrange("p g t -> p (g t)"), start=True, stop=True) \
                    .then_inc(filled[b], 1)

            def times_v(qh, u, c):
                place = ring_place(G * c + G - 1, isinstance(u, int) and u == NU - 1)
                i = place % len(SCORE_BANKS)
                b = SCORE_BANKS[i]
                pe.wait_ge(drained[b], base[b] + u * RING_USES + ring_fills(place, i))
                if c == 0:
                    pe.wait_ge(v_slot_ready, u + 1)
                    pe.wait_ge(drained[PV_BANK], base[PV_BANK] + u)
                for j in range(G):
                    ins = pe.matmul(ps[32 * j:32 * j + 32, PV_BANK, :], v_slot[:, qh, c, j, :], pbuf[:, c % 2, j, :],
                                    start=(c == 0), stop=(c == TT - 1))
                ins.then_inc(pv_chunk if c < TT - 1 else filled[PV_BANK], 1)

            pe.wait_ge(k_packed[0], 48)
            pe.wait_ge(q_packed[0], 48)
            side = [key for key in beside_max_pass() if key[0] != "shift"]
            for k in range(FILLS):
                max_tile(0, 0, 0, k)
                if k % 2 == 0 or k > FILLS - 2:
                    key = side.pop(0)
                    setup[key[0]](key)
            pe.wait_ge(q_packed[1], 48)
            for k in range(LEAD):
                max_tile(0, 1, 1, k)
                if k == 0:
                    pe.wait_ge(consts, 5)
                    shift_rows(0)
                if k == LEAD - 3:
                    pe.wait_ge(ones_rows_in, 48)
                    pe.wait_ge(shift_landed, 48)
                if k >= LEAD - 3 and k < LEAD - 1:
                    score_tile(0, 0, 0, k - (LEAD - 3))
            pe.wait_ge(k_packed[1], 48)
            pe.wait_ge(q_packed[2], 48)

            def unit(g, qh, u, nxt, after):
                fill = LEAD
                for s in range(2, STEPS + 2):
                    if s == SHIFT_AT and nxt is not None:
                        shift_rows(nxt[2])
                    if s < STEPS:
                        score_tile(g, qh, u, s)
                    elif nxt is not None:
                        if s == STEPS:
                            pe.wait_ge(shift_landed, (u + 2) * 48)
                        score_tile(*nxt, s - STEPS)
                    if s % 2 == 1:
                        if fill < FILLS and nxt is not None:
                            max_tile(*nxt, fill)
                        elif fill >= FILLS and after is not None:
                            max_tile(*after, fill - FILLS)
                        fill += 1
                    if s % G == 1 and s > G:
                        times_v(qh, u, s // G - 1)

            with pe.Fori(0, NG - 1) as g:
                unit(g, 0, g * 2, (g, 1, g * 2 + 1), (g + 1, 0, g * 2 + 2))
                unit(g, 1, g * 2 + 1, (g + 1, 0, g * 2 + 2), (g + 1, 1, g * 2 + 3))
                for s in (k_packed[2], q_packed[3], q_packed[4]):
                    pe.wait_ge(s, 48)
            unit(NG - 1, 0, NU - 2, (NG - 1, 1, NU - 1), None)
            def w_transposed(key):
                n, second = divmod(key[1], 2)
                if key[1] == 0:
                    pe.wait_ge(tern_ready, 8)
                (w2_transposed if second else w1_transposed)(key, n)

            def w1_transposed(key, c):
                out = to_fill(pe, key).bitcast(BF16)
                for f in range(FC):
                    ins = pe.transpose(out[:, P * f:P * f + P], tern1[:, f, P * c:P * c + P], identb[:, :])
                ins.then_inc(fill_sem(key), 1)

            def w2_transposed(key, n):
                out = to_fill(pe, key).bitcast(BF16)
                for f in range(4):
                    for c in range(DC):
                        ins = pe.transpose(out[:, D * f + P * c:D * f + P * c + P],
                                           tern2[:, c, P * (4 * n + f):P * (4 * n + f) + P], identb[:, :])
                ins.then_inc(fill_sem(key), 1)

            def o_to_tokens(key):
                t = key[1]
                if t % 4 == 0:
                    pe.wait_ge(drained[PV_BANK], base[PV_BANK] + NU - 1 + t // 4)
                out = to_fill(pe, key)
                for g in range(NG):
                    ins = pe.transpose(out[:, P * g:P * g + P], o_un[:, g, P * t:P * t + P], ident[:, :])
                ins.then_inc(fill_sem(key), 1)

            def o_to_features(key):
                _, which, t = key
                n = number[key]
                if which == "a":
                    is_drained(pe, ("ao_t", t))
                else:
                    pe.wait_ge(divided, t + 1)
                out = to_fill(pe, key)
                for c in range(DC):
                    ins = pe.transpose(out[:, P * c:P * c + P], o_norm[:, n % 2, P * c:P * c + P], ident[:, :])
                ins.then_inc(fill_sem(key), 1)

            def project_o(key):
                which, t = ("a" if key[0] == "ao_y" else "b"), key[1]
                is_drained(pe, ("o", which, t))
                if which == "b" and t == 0:
                    pe.wait_ge(wout_in, 16)
                w = wT[:, O_, :, :] if which == "a" else w_out
                out = to_fill(pe, key)[:, 0:D]
                add_bias(out, "bo" if which == "a" else "bout")
                for c in range(DC):
                    ins = pe.matmul(out, oT[:, number["o", which, t] % 2, c, :], w[:, c, :], start=False,
                                    stop=(c == DC - 1))
                ins.then_inc(fill_sem(key), 1)

            def hidden(key):
                _, r, s, f = key
                first, n = RANGES[r][s]
                v = tokens(r, s)
                if f == 0:
                    for p in range(first // 2, (first + n) // 2):
                        is_drained(pe, ("lnt", 2 * r + 1, p))
                    is_drained(pe, ("w", 2))
                out = to_fill(pe, key)[:, 0:v.stop - v.start]
                for part in (0, 1):
                    for c in range(DC):
                        ins = pe.matmul(out, w1T[:, c, P * f:P * f + P], x12[:, part, c, v],
                                        start=(part == 0 and c == 0), stop=(part == 1 and c == DC - 1))
                ins.then_inc(fill_sem(key), 1)

            def add_hidden(r, p, f):
                for t in (2 * p, 2 * p + 1):
                    out = bank(("y", r, p))[:, D * (t % 2):D * (t % 2) + D]
                    for n in range(NPART):
                        ins = pe.matmul(out, g_parts[:, n, f, P * t:P * t + P], w2T[:, f, :],
                                        start=False, stop=(f == FC - 1 and n == NPART - 1 and t % 2 == 1))
                return ins

            def ffn_out_part(r, s, f):
                pe.wait_ge(g3_ready, number["h", r, s, f] + 1)
                if f == 0:
                    is_drained(pe, ("w", 3))
                first, n = RANGES[r][s]
                for p in range(first // 2, (first + n) // 2):
                    if f == 0:
                        at = BIAS_AT["b2"]
                        pe.matmul(to_fill(pe, ("y", r, p)).rearrange("p (t d) -> p t d", t=2), onesb[0:NPART, 0:P],
                                  bias_rows[:, at:at + D].unsqueeze(1).broadcast_to([NPART, 2, D]), start=True, stop=False)
                    add_hidden(r, p, f)

            def ffn_out(key):
                _, r, p = key
                s = range_of(r, 2 * p)
                for f in range(Y_LAST, FC):
                    if 2 * p == RANGES[r][s][0]:
                        pe.wait_ge(g3_ready, number["h", r, s, f] + 1)
                    ins = add_hidden(r, p, f)
                ins.then_inc(fill_sem(key), 1)

            def heads_qk(key):
                t = key[1]
                is_drained(pe, ("lnt", 2, t // 2))
                if t == 0:
                    pe.wait_ge(wqkv_in, 16)
                add_bias(to_fill(pe, key), "qk")
                out = bank(key).rearrange("p (h n) -> p h n", h=H)
                for d in range(DC):
                    ins = pe.matmul(out, xT[:, d, P * t:P * t + P],
                                    wqkv[:, d, :].rearrange("p (h n) -> p h n", h=H)[:, :, 0:2 * HD],
                                    start=False, stop=(d == DC - 1))
                ins.then_inc(fill_sem(key), 1)

            def heads_v_sum(key):
                t = key[1]
                if t == 0:
                    pe.wait_ge(vsum_ready, 1)
                out = to_fill(pe, key)[:, 0:HD]
                pe.matmul(out, ones[0:1, :], b_vsum[:, :], start=True, stop=False)
                for d in range(DC):
                    ins = pe.matmul(out, xT[:, d, P * t:P * t + P], w_vsum[:, d, :], start=False, stop=(d == DC - 1))
                ins.then_inc(fill_sem(key), 1)

            tail = {"w": w_transposed, "ao_t": o_to_tokens, "o": o_to_features, "ao_y": project_o,
                    "lnt": transpose_pair, "h": hidden, "y": ffn_out, "qk": heads_qk, "vs": heads_v_sum,
                    "bo_y": project_o}
            for e in events:
                if e[0] == "score":
                    score_tile(NG - 1, 1, NU - 1, e[1])
                if e[0] == "pv":
                    times_v(1, NU - 1, e[1])
                if e[0] == "y_part":
                    ffn_out_part(*e[1:])
                if e[0] in TAIL_FILLS:
                    tail[e[0]](e)


_INS = ["L0_attn_a_x", *[f"L0_attn_a_{w}{m}" for m in "qkvo" for w in "WbBA"], "L0_attn_b_Wqkv", "L0_attn_b_bqkv",
        "L0_attn_b_Wout", "L0_attn_b_bout", "L0_ffn_w1", "L0_ffn_b1", "L0_ffn_w2", "L0_ffn_b2"]


def kernel(**inputs):
    import numpy as _np
    import concourse.bacc as _bacc
    from concourse import mybir as _mybir
    from concourse.bass_utils import run_bass_kernel_spmd as _run

    nc = _bacc.Bacc("TRN2", target_bir_lowering=False, num_devices=1)
    arrays, aps = {}, {}
    for name in _INS:
        v = _np.ascontiguousarray(inputs[name])
        arrays[f"in_{name}_dram"] = v
        aps[name] = nc.dram_tensor(f"in_{name}_dram", v.shape, _mybir.dt.from_np(v.dtype), kind="ExternalInput").ap()
    aps["out"] = nc.dram_tensor("out_dram", (1, T, D), F32, kind="ExternalOutput").ap()
    build(nc, aps)
    r = _run(nc, [arrays], core_ids=[0])
    return r.results[0]["out_dram"]
```
